# Optimizing a Trainium2 kernel written in Bass

```python
import numpy as np
import jax
import jax.numpy as jnp

def _softmax(x, axis=-1):
    return jax.nn.softmax(x, axis=axis)

def _gelu(x):
    return jax.nn.gelu(x, approximate=True)

def _silu(x):
    return jax.nn.silu(x)

def _sigmoid(x):
    return jax.nn.sigmoid(x)

def _layernorm(x, axis=-1, eps=1e-05):
    m = jnp.mean(x, axis=axis, keepdims=True)
    v = jnp.var(x, axis=axis, keepdims=True)
    return (x - m) / jnp.sqrt(v + eps)

def _scatter_add(tgt, idx, src, axis=0):
    return tgt.at[idx].add(src)

def _segment_sum(src, seg, n):
    return jax.ops.segment_sum(src, seg, n)
kernel_name = 'mk_dlrm_tower_d1_rec_r8_18ee69'

def setup_inputs(seed: int=0):
    np.random.seed(seed)
    _w = jnp.asarray

    def _rec_inputs():
        import jax
        import jax.numpy as jnp
        _tk = jax.random.key(seed)
        dense_ctx = jax.random.normal(jax.random.fold_in(_tk, 190), (1024, 16), jnp.float32)
        ids = jnp.stack([jax.random.randint(jax.random.fold_in(_tk, 200 + f), (1024,), 0, v, jnp.int32) for f, v in enumerate([12500, 1250, 12500, 12500, 12500, 125000, 1250, 1250, 1000, 1000, 12500, 1250, 1250, 12500, 12500, 12500, 12500, 125000, 125000, 1000, 1000, 1250, 1000, 1000, 12500, 12500, 125000, 1250, 12500, 1250, 1250, 1250, 125000, 125000, 12500, 12500, 125000, 125000, 12500])], axis=1)
        tbl_0 = 0.05 * jax.random.normal(jax.random.fold_in(_tk, 500 + 0), (12500, 16), jnp.float32)
        tbl_1 = 0.05 * jax.random.normal(jax.random.fold_in(_tk, 500 + 1), (1250, 16), jnp.float32)
        tbl_2 = 0.05 * jax.random.normal(jax.random.fold_in(_tk, 500 + 2), (12500, 16), jnp.float32)
        tbl_3 = 0.05 * jax.random.normal(jax.random.fold_in(_tk, 500 + 3), (12500, 16), jnp.float32)
        tbl_4 = 0.05 * jax.random.normal(jax.random.fold_in(_tk, 500 + 4), (12500, 16), jnp.float32)
        tbl_5 = 0.05 * jax.random.normal(jax.random.fold_in(_tk, 500 + 5), (125000, 16), jnp.float32)
        tbl_6 = 0.05 * jax.random.normal(jax.random.fold_in(_tk, 500 + 6), (1250, 16), jnp.float32)
        tbl_7 = 0.05 * jax.random.normal(jax.random.fold_in(_tk, 500 + 7), (1250, 16), jnp.float32)
        tbl_8 = 0.05 * jax.random.normal(jax.random.fold_in(_tk, 500 + 8), (1000, 16), jnp.float32)
        tbl_9 = 0.05 * jax.random.normal(jax.random.fold_in(_tk, 500 + 9), (1000, 16), jnp.float32)
        tbl_10 = 0.05 * jax.random.normal(jax.random.fold_in(_tk, 500 + 10), (12500, 16), jnp.float32)
        tbl_11 = 0.05 * jax.random.normal(jax.random.fold_in(_tk, 500 + 11), (1250, 16), jnp.float32)
        tbl_12 = 0.05 * jax.random.normal(jax.random.fold_in(_tk, 500 + 12), (1250, 16), jnp.float32)
        tbl_13 = 0.05 * jax.random.normal(jax.random.fold_in(_tk, 500 + 13), (12500, 16), jnp.float32)
        tbl_14 = 0.05 * jax.random.normal(jax.random.fold_in(_tk, 500 + 14), (12500, 16), jnp.float32)
        tbl_15 = 0.05 * jax.random.normal(jax.random.fold_in(_tk, 500 + 15), (12500, 16), jnp.float32)
        tbl_16 = 0.05 * jax.random.normal(jax.random.fold_in(_tk, 500 + 16), (12500, 16), jnp.float32)
        tbl_17 = 0.05 * jax.random.normal(jax.random.fold_in(_tk, 500 + 17), (125000, 16), jnp.float32)
        tbl_18 = 0.05 * jax.random.normal(jax.random.fold_in(_tk, 500 + 18), (125000, 16), jnp.float32)
        tbl_19 = 0.05 * jax.random.normal(jax.random.fold_in(_tk, 500 + 19), (1000, 16), jnp.float32)
        tbl_20 = 0.05 * jax.random.normal(jax.random.fold_in(_tk, 500 + 20), (1000, 16), jnp.float32)
        tbl_21 = 0.05 * jax.random.normal(jax.random.fold_in(_tk, 500 + 21), (1250, 16), jnp.float32)
        tbl_22 = 0.05 * jax.random.normal(jax.random.fold_in(_tk, 500 + 22), (1000, 16), jnp.float32)
        tbl_23 = 0.05 * jax.random.normal(jax.random.fold_in(_tk, 500 + 23), (1000, 16), jnp.float32)
        tbl_24 = 0.05 * jax.random.normal(jax.random.fold_in(_tk, 500 + 24), (12500, 16), jnp.float32)
        tbl_25 = 0.05 * jax.random.normal(jax.random.fold_in(_tk, 500 + 25), (12500, 16), jnp.float32)
        tbl_26 = 0.05 * jax.random.normal(jax.random.fold_in(_tk, 500 + 26), (125000, 16), jnp.float32)
        tbl_27 = 0.05 * jax.random.normal(jax.random.fold_in(_tk, 500 + 27), (1250, 16), jnp.float32)
        tbl_28 = 0.05 * jax.random.normal(jax.random.fold_in(_tk, 500 + 28), (12500, 16), jnp.float32)
        tbl_29 = 0.05 * jax.random.normal(jax.random.fold_in(_tk, 500 + 29), (1250, 16), jnp.float32)
        tbl_30 = 0.05 * jax.random.normal(jax.random.fold_in(_tk, 500 + 30), (1250, 16), jnp.float32)
        tbl_31 = 0.05 * jax.random.normal(jax.random.fold_in(_tk, 500 + 31), (1250, 16), jnp.float32)
        tbl_32 = 0.05 * jax.random.normal(jax.random.fold_in(_tk, 500 + 32), (125000, 16), jnp.float32)
        tbl_33 = 0.05 * jax.random.normal(jax.random.fold_in(_tk, 500 + 33), (125000, 16), jnp.float32)
        tbl_34 = 0.05 * jax.random.normal(jax.random.fold_in(_tk, 500 + 34), (12500, 16), jnp.float32)
        tbl_35 = 0.05 * jax.random.normal(jax.random.fold_in(_tk, 500 + 35), (12500, 16), jnp.float32)
        tbl_36 = 0.05 * jax.random.normal(jax.random.fold_in(_tk, 500 + 36), (125000, 16), jnp.float32)
        tbl_37 = 0.05 * jax.random.normal(jax.random.fold_in(_tk, 500 + 37), (125000, 16), jnp.float32)
        tbl_38 = 0.05 * jax.random.normal(jax.random.fold_in(_tk, 500 + 38), (12500, 16), jnp.float32)
        _rk = jax.random.fold_in(_tk, 7)
        W_top1 = 0.05 * jax.random.normal(jax.random.fold_in(_tk, 801), (400, 512), jnp.float32)
        W_top2 = 0.0441942 * jax.random.normal(jax.random.fold_in(_tk, 802), (512, 256), jnp.float32)
        W_top3 = 0.0625 * jax.random.normal(jax.random.fold_in(_tk, 803), (256, 1), jnp.float32)
        b_top1 = jnp.zeros((512,), jnp.float32)
        b_top2 = jnp.zeros((256,), jnp.float32)
        return (dense_ctx, ids, tbl_0, tbl_1, tbl_2, tbl_3, tbl_4, tbl_5, tbl_6, tbl_7, tbl_8, tbl_9, tbl_10, tbl_11, tbl_12, tbl_13, tbl_14, tbl_15, tbl_16, tbl_17, tbl_18, tbl_19, tbl_20, tbl_21, tbl_22, tbl_23, tbl_24, tbl_25, tbl_26, tbl_27, tbl_28, tbl_29, tbl_30, tbl_31, tbl_32, tbl_33, tbl_34, tbl_35, tbl_36, tbl_37, tbl_38, W_top1, b_top1, W_top2, b_top2, W_top3)
    dense_ctx, ids, tbl_0, tbl_1, tbl_2, tbl_3, tbl_4, tbl_5, tbl_6, tbl_7, tbl_8, tbl_9, tbl_10, tbl_11, tbl_12, tbl_13, tbl_14, tbl_15, tbl_16, tbl_17, tbl_18, tbl_19, tbl_20, tbl_21, tbl_22, tbl_23, tbl_24, tbl_25, tbl_26, tbl_27, tbl_28, tbl_29, tbl_30, tbl_31, tbl_32, tbl_33, tbl_34, tbl_35, tbl_36, tbl_37, tbl_38, W_top1, b_top1, W_top2, b_top2, W_top3 = _rec_inputs()

    def _L0_rec_setup():
        import jax, jax.numpy as jnp
        import numpy as np
        B, F0, D = (256, 39, 16)
        CROSS = [128, 128, 128]
        key = jax.random.key(seed)
        k0, k1, k2, k3 = jax.random.split(key, 4)
        inputs = jax.random.normal(k0, (B, F0, D), dtype=jnp.float32)
        f0 = jax.random.normal(k1, (F0 * F0, CROSS[0]), dtype=jnp.float32) * 0.05
        f1 = jax.random.normal(k2, (CROSS[0] * F0, CROSS[1]), dtype=jnp.float32) * 0.05
        f2 = jax.random.normal(k3, (CROSS[1] * F0, CROSS[2]), dtype=jnp.float32) * 0.05
        return {'inputs': inputs, 'f0': f0, 'f1': f1, 'f2': f2}
    _L0_rec_all = _L0_rec_setup()
    _L0_rec_in = {k: v for k, v in _L0_rec_all.items() if k in ('f0', 'f1', 'f2')}
    del _L0_rec_all
    return {'dense_ctx': dense_ctx, 'ids': ids, 'tbl_0': tbl_0, 'tbl_1': tbl_1, 'tbl_2': tbl_2, 'tbl_3': tbl_3, 'tbl_4': tbl_4, 'tbl_5': tbl_5, 'tbl_6': tbl_6, 'tbl_7': tbl_7, 'tbl_8': tbl_8, 'tbl_9': tbl_9, 'tbl_10': tbl_10, 'tbl_11': tbl_11, 'tbl_12': tbl_12, 'tbl_13': tbl_13, 'tbl_14': tbl_14, 'tbl_15': tbl_15, 'tbl_16': tbl_16, 'tbl_17': tbl_17, 'tbl_18': tbl_18, 'tbl_19': tbl_19, 'tbl_20': tbl_20, 'tbl_21': tbl_21, 'tbl_22': tbl_22, 'tbl_23': tbl_23, 'tbl_24': tbl_24, 'tbl_25': tbl_25, 'tbl_26': tbl_26, 'tbl_27': tbl_27, 'tbl_28': tbl_28, 'tbl_29': tbl_29, 'tbl_30': tbl_30, 'tbl_31': tbl_31, 'tbl_32': tbl_32, 'tbl_33': tbl_33, 'tbl_34': tbl_34, 'tbl_35': tbl_35, 'tbl_36': tbl_36, 'tbl_37': tbl_37, 'tbl_38': tbl_38, 'W_top1': W_top1, 'b_top1': b_top1, 'W_top2': W_top2, 'b_top2': b_top2, 'W_top3': W_top3, 'L0_rec_f0': _L0_rec_in['f0'], 'L0_rec_f1': _L0_rec_in['f1'], 'L0_rec_f2': _L0_rec_in['f2']}

def reference(dense_ctx, ids, tbl_0, tbl_1, tbl_2, tbl_3, tbl_4, tbl_5, tbl_6, tbl_7, tbl_8, tbl_9, tbl_10, tbl_11, tbl_12, tbl_13, tbl_14, tbl_15, tbl_16, tbl_17, tbl_18, tbl_19, tbl_20, tbl_21, tbl_22, tbl_23, tbl_24, tbl_25, tbl_26, tbl_27, tbl_28, tbl_29, tbl_30, tbl_31, tbl_32, tbl_33, tbl_34, tbl_35, tbl_36, tbl_37, tbl_38, W_top1, b_top1, W_top2, b_top2, W_top3, L0_rec_f0, L0_rec_f1, L0_rec_f2):
    import jax
    import jax.numpy as jnp

    def _L0_rec_ref(inputs, f0, f1, f2):
        import jax, jax.numpy as jnp
        import numpy as np
        B, F0, D = (256, 39, 16)
        CROSS = [128, 128, 128]
        filters = [f0, f1, f2]
        x0 = inputs
        xk = inputs
        outs = []
        for W in filters:
            b, f, d = x0.shape
            g = xk.shape[1]
            z = jnp.einsum('bfd,bgd->bfgd', x0, xk).reshape(b, f * g, d)
            cur = jnp.einsum('bpd,pm->bmd', z, W)
            outs.append(cur)
            xk = cur
        result = jnp.concatenate(outs, axis=1)
        return jnp.sum(result, axis=-1)
    e = jnp.stack([tbl_0[ids[:, 0]], tbl_1[ids[:, 1]], tbl_2[ids[:, 2]], tbl_3[ids[:, 3]], tbl_4[ids[:, 4]], tbl_5[ids[:, 5]], tbl_6[ids[:, 6]], tbl_7[ids[:, 7]], tbl_8[ids[:, 8]], tbl_9[ids[:, 9]], tbl_10[ids[:, 10]], tbl_11[ids[:, 11]], tbl_12[ids[:, 12]], tbl_13[ids[:, 13]], tbl_14[ids[:, 14]], tbl_15[ids[:, 15]], tbl_16[ids[:, 16]], tbl_17[ids[:, 17]], tbl_18[ids[:, 18]], tbl_19[ids[:, 19]], tbl_20[ids[:, 20]], tbl_21[ids[:, 21]], tbl_22[ids[:, 22]], tbl_23[ids[:, 23]], tbl_24[ids[:, 24]], tbl_25[ids[:, 25]], tbl_26[ids[:, 26]], tbl_27[ids[:, 27]], tbl_28[ids[:, 28]], tbl_29[ids[:, 29]], tbl_30[ids[:, 30]], tbl_31[ids[:, 31]], tbl_32[ids[:, 32]], tbl_33[ids[:, 33]], tbl_34[ids[:, 34]], tbl_35[ids[:, 35]], tbl_36[ids[:, 36]], tbl_37[ids[:, 37]], tbl_38[ids[:, 38]]], axis=1)
    z = _L0_rec_ref(e, L0_rec_f0, L0_rec_f1, L0_rec_f2)
    z = z.reshape(z.shape[0], -1)
    h = jnp.concatenate([z, dense_ctx], axis=1)
    h = jnp.maximum(h @ W_top1 + b_top1, 0.0)
    h = jnp.maximum(h @ W_top2 + b_top2, 0.0)
    y = h @ W_top3
    return y

_drawn_inputs = setup_inputs


def setup_inputs(seed=0):
    import zlib

    import numpy as np

    out = dict(_drawn_inputs(seed))
    spreads = {'b_top1': (0.0, 0.531), 'b_top2': (0.0, 0.1)}
    factors = {'tbl_0': 4.386,
     'tbl_1': 4.922,
     'tbl_2': 4.596,
     'tbl_3': 4.786,
     'tbl_4': 4.935,
     'tbl_5': 4.839,
     'tbl_6': 4.568,
     'tbl_7': 4.509,
     'tbl_8': 4.732,
     'tbl_9': 4.666,
     'tbl_10': 4.965,
     'tbl_11': 4.659,
     'tbl_12': 3.94,
     'tbl_13': 4.541,
     'tbl_14': 4.422,
     'tbl_15': 4.863,
     'tbl_16': 5.297,
     'tbl_17': 4.686,
     'tbl_18': 5.057,
     'tbl_19': 4.886,
     'tbl_20': 4.94,
     'tbl_21': 4.596,
     'tbl_22': 4.48,
     'tbl_23': 4.731,
     'tbl_24': 4.518,
     'tbl_25': 4.591,
     'tbl_26': 4.713,
     'tbl_27': 4.85,
     'tbl_28': 4.819,
     'tbl_29': 4.841,
     'tbl_30': 4.814,
     'tbl_31': 4.549,
     'tbl_32': 4.706,
     'tbl_33': 4.787,
     'tbl_34': 4.576,
     'tbl_35': 4.564,
     'tbl_36': 4.758,
     'tbl_37': 4.677,
     'tbl_38': 4.989,
     'L0_rec_f1': 4.968,
     'L0_rec_f2': 8.0}
    for name, (base, spread) in spreads.items():
        noise = np.random.default_rng([zlib.crc32(name.encode()), seed]).standard_normal(out[name].shape)
        drawn = base * np.exp(spread * noise) if base else spread * noise
        out[name] = jnp.asarray(drawn.astype(out[name].dtype))
    for name, factor in factors.items():
        out[name] = (out[name] * factor).astype(out[name].dtype)
    return out
```

```python
import concourse.bass as bass
from concourse import mybir
from contextlib import ExitStack

F32 = mybir.dt.float32
F32R = mybir.dt.float32r
I32 = mybir.dt.int32
ALU = mybir.AluOpType
ACT = mybir.ActivationFunctionType
AX = mybir.AxisListType

BATCH = 1024
FIELDS = 39
DIM = 16
CROSS = 128
DENSE = 16
HID1 = 512
HID2 = 256

TILE_B = 128
TILES = BATCH // TILE_B
TILE_COLS = TILE_B * DIM
GROUP_COLS = 512
GROUPS = TILE_COLS // GROUP_COLS
ROWS = 128
SLOTS = TILE_COLS // ROWS
SLOTS_G = SLOTS // GROUPS
SLOT_B = ROWS // DIM

SHIFTS = (FIELDS + 1) // 2
PER_TILE = 3
PAIR_TILES = -(-SHIFTS // PER_TILE)
PAIR_ROWS = PER_TILE * FIELDS

UNITS = -(-FIELDS // 4)
RING = 5
VECTOR_UNITS = (2, 5, 8)
SCALAR_UNITS = tuple(u for u in range(UNITS) if u not in VECTOR_UNITS)
EMB_TURN_AFTER = (1, 3, 5, 7)
EMB_COPY_AFTER = (1, 3, 6, 7)
LAG = 2
PAIR_RING = 4
X2_RING = 4


def unit_fields(u):
    return 4 * u, min(4 * u + 4, FIELDS)


def shifts_of(k):
    return range(PER_TILE * k, min(PER_TILE * k + PER_TILE, SHIFTS))


def pair_rows(k):
    return len(shifts_of(k)) * FIELDS


def cin_tower(nc, ids, tables, ident, block_mask, w0a, w0b, w1, w2, dense_t, wt1, wt1d, bt1, wt2, bt2, wt3, out):
    with ExitStack() as ctx:
        def sb(name, shape, dt=F32):
            return ctx.enter_context(nc.sbuf_tensor(name, shape, dt))

        def bank(name):
            return ctx.enter_context(nc.psum_tensor(name, [128, 512], F32))

        def sem(name):
            return ctx.enter_context(nc.semaphore(name))

        eye = sb("eye", [128, 128])
        mask = sb("mask", [128, SLOT_B])
        W0 = sb("W0", [PAIR_ROWS, PAIR_TILES, CROSS])
        W1h = sb("W1h", [128, FIELDS * CROSS], F32R)
        W1l = sb("W1l", [128, FIELDS * CROSS], F32R)
        W2 = sb("W2", [128, FIELDS, CROSS])
        BT1 = sb("BT1", [128, HID1 // 128])
        BT2 = sb("BT2", [128, HID2 // 128])
        WT3 = sb("WT3", [128, HID2 // 128])
        idx = sb("idx", [128, FIELDS], I32)
        emb = sb("emb", [128, PER_TILE * FIELDS * DIM])
        x0T = sb("x0T", [PAIR_ROWS, TILE_COLS])
        shifted = sb("shifted", [128, 2, PAIR_TILES, GROUP_COLS])
        pairs = sb("pairs", [PAIR_ROWS, PAIR_RING, GROUP_COLS])
        x0r = sb("x0r", [128, 2, SLOTS_G, FIELDS + 1])
        x1h = sb("x1h", [128, 2, GROUP_COLS], F32R)
        x1l = sb("x1l", [128, 2, GROUP_COLS], F32R)
        scaled = sb("scaled", [128, 2, FIELDS, CROSS])
        x2 = sb("x2", [128, X2_RING, CROSS])
        spread = sb("spread", [128, X2_RING, FIELDS + 1, SLOT_B])
        gram = sb("gram", [128, FIELDS + 1, TILE_B])
        S = sb("S", [128, 3, BATCH])

        tower = shifted[:].rearrange("p a k c -> p (a k) c")
        WT1 = tower[:, 0:3, :]
        WT1d = tower[0:DENSE, 3, :]
        WT2 = tower[:, 4:6, :].rearrange("p k (c m) -> p (k c) m", m=HID2)
        denseT = tower[0:DENSE, 6:8, :].rearrange("p a b -> p (a b)")
        hid1 = scaled[:, 0, 0:HID1 // 128 * 8, :].rearrange("p (k c) m -> p k (c m)", k=HID1 // 128)
        hid2 = scaled[:, 1, 0:HID2 // 128 * 8, :].rearrange("p (k c) m -> p k (c m)", k=HID2 // 128)
        y_row = pairs[0:1, 0:2, :].rearrange("p a b -> p (a b)")

        ring = [bank(f"ring{i}") for i in range(RING)]
        x1_ps = bank("x1_ps")
        misc_ps = bank("misc_ps")
        gram_ps = bank("gram_ps")

        weights_in = sem("weights_in")
        tower_in = sem("tower_in")
        w1_in = sem("w1_in")
        w1_high = sem("w1_high")
        w1_low = sem("w1_low")
        w0_summed = sem("w0_summed")
        ones_set = sem("ones_set")
        idx_in = sem("idx_in")
        gathered = sem("gathered")
        emb_copied = sem("emb_copied")
        emb_turned = sem("emb_turned")
        x0T_copied = sem("x0T_copied")
        shifted_in = [sem("shifted_in0"), sem("shifted_in1")]
        x0r_turned = sem("x0r_turned")
        x0r_copied = sem("x0r_copied")
        pairs_made = sem("pairs_made")
        pairs_used = sem("pairs_used")
        x1_high = sem("x1_high")
        x1_low = sem("x1_low")
        unit_made = sem("unit_made")
        scalar_scaled = sem("scalar_scaled")
        vector_scaled = sem("vector_scaled")
        x2_summed = sem("x2_summed")
        spread_made = sem("spread_made")
        gram_made = sem("gram_made")
        gram_copied = sem("gram_copied")
        s3_made = sem("s3_made")
        s3_copied = sem("s3_copied")
        hid1_made = sem("hid1_made")
        hid1_copied = sem("hid1_copied")
        hid2_made = sem("hid2_made")
        hid2_copied = sem("hid2_copied")
        y_made = sem("y_made")
        y_copied = sem("y_copied")
        y_out = sem("y_out")

        NS = len(SCALAR_UNITS)
        NV = len(VECTOR_UNITS)

        def scaled_before(u, slot):
            if u in VECTOR_UNITS:
                return vector_scaled, slot * NV + VECTOR_UNITS.index(u) + 1
            return scalar_scaled, slot * NS + SCALAR_UNITS.index(u) + 1

        def tiles(eng, body):
            body(0, True, False)
            with eng.Fori(1, TILES - 1) as t:
                body(t, False, False)
            body(TILES - 1, False, True)

        block = ctx.enter_context(nc.Block())

        @block.sync
        def _(sp):
            sp.dma_start(eye[:], ident).then_inc(weights_in, 16)
            sp.dma_start(mask[:], block_mask).then_inc(weights_in, 16)
            sp.dma_start(W0[:], w0a).then_inc(weights_in, 16)
            sp.dma_start(shifted[0:PAIR_ROWS, 1, :, 0:CROSS], w0b).then_inc(weights_in, 16)
            sp.dma_start(W2[:], w1).then_inc(w1_in, 16)

            def shift_group(t, g):
                n = t * GROUPS + g
                p = g % 2
                if g == 0:
                    sp.wait_ge(x0T_copied, (t + 1) * 4)
                elif not (isinstance(n, int) and n < 2):
                    sp.wait_ge(pairs_made, (n - 1) * PAIR_TILES)
                else:
                    sp.wait_ge(w0_summed, 1)
                for k in range(PAIR_TILES):
                    for i, s in enumerate(shifts_of(k)):
                        sp.dma_start(shifted[i * FIELDS:(i + 1) * FIELDS, p, k, :],
                                     x0T[s:s + FIELDS, g * GROUP_COLS:(g + 1) * GROUP_COLS]
                                     ).then_inc(shifted_in[p], 16)

            def body(t, first, last):
                for g in range(GROUPS):
                    shift_group(t, g)
                    if first and g == 0:
                        sp.wait_ge(w1_low, 1)
                        sp.dma_start(W2[:], w2).then_inc(w1_in, 16)

            tiles(sp, body)
            sp.wait_ge(pairs_made, TILES * GROUPS * PAIR_TILES)
            for dst, src in ((WT1, wt1), (WT1d, wt1d), (BT1[:], bt1), (WT2, wt2), (BT2[:], bt2), (WT3[:], wt3),
                             (denseT, dense_t)):
                sp.dma_start(dst, src).then_inc(tower_in, 16)
            sp.wait_ge(y_copied, 2)
            sp.dma_start(out, y_row).then_inc(y_out, 16)
            sp.wait_ge(y_out, 16)

        @block.gpsimd
        def _(pool):
            def load_idx(t):
                if not isinstance(t, int) or t > 0:
                    pool.wait_ge(gathered, t * FIELDS * 16)
                pool.dma_start(idx[:], ids[:, bass.ds(t, 1), :].rearrange("p t f -> p (t f)")
                               if not isinstance(t, int) else ids[:, t, :]).then_inc(idx_in, 16)

            def idx_loaded(t):
                pool.wait_ge(idx_in, (t + 1) * 16)

            def rows_gathered(t):
                pool.wait_ge(gathered, (t + 1) * FIELDS * 16)

            def gather(t, fields):
                for f in fields:
                    pool.indirect_dma_start(
                        emb[:, f * DIM:(f + 1) * DIM], None, tables[f],
                        bass.IndirectOffsetOnAxis(ap=idx[:, f:f + 1], axis=0)).then_inc(gathered, 16)

            def triple(t):
                for c in range(1, PER_TILE):
                    pool.tensor_copy(emb[:, c * FIELDS * DIM:(c + 1) * FIELDS * DIM],
                                     emb[:, 0:FIELDS * DIM]).then_inc(emb_copied, 1)

            def make_spread(t, i):
                slot = t * SLOTS + i
                g, j = divmod(i, SLOTS_G)
                if j == 0:
                    pool.wait_ge(x0r_copied, t * GROUPS + g + 1)
                if not isinstance(slot, int) or slot >= X2_RING:
                    pool.wait_ge(gram_made, slot - X2_RING + 1)
                pool.tensor_tensor(
                    spread[:, i % X2_RING, :, :],
                    x0r[:, g % 2, j, :].unsqueeze(2).to_broadcast([128, FIELDS + 1, SLOT_B]),
                    mask[:].unsqueeze(1).to_broadcast([128, FIELDS + 1, SLOT_B]),
                    ALU.mult).then_inc(spread_made, 1)

            load_idx(0)
            idx_loaded(0)
            gather(0, range(FIELDS))
            rows_gathered(0)
            triple(0)
            pool.wait_ge(weights_in, 64)
            pool.wait_ge(ones_set, 1)

            def body(t, first, last):
                for i in range(SLOTS):
                    if i == 1 and not last:
                        idx_loaded(t + 1)
                    if i == 11 and not last:
                        rows_gathered(t + 1)
                    make_spread(t, i)
                    if last:
                        continue
                    if i == 0:
                        pool.wait_ge(emb_turned, (t + 1) * 4)
                        load_idx(t + 1)
                    if 1 <= i < 11:
                        gather(t + 1, range(4 * i - 4, min(4 * i, FIELDS)))
                    if i == 11:
                        triple(t + 1)

            tiles(pool, body)

        @block.scalar
        def _(act):
            act.wait_ge(w1_in, 16)
            nc.scalar.activation(W1h[:], W2[:].rearrange("p f m -> p (f m)"), ACT.Copy).then_inc(w1_high, 1)

            def copy_x0T(t, rounds=range(4)):
                for r in rounds:
                    act.wait_ge(emb_turned, t * 4 + r + 1)
                    if r == 0 and not (isinstance(t, int) and t == 0):
                        act.wait_ge(pairs_made, t * GROUPS * PAIR_TILES)
                        act.wait_ge(x0r_turned, t * GROUPS)
                    nc.scalar.activation(
                        x0T[:].rearrange("f (b d) -> f d b", d=DIM)[:, 4 * r:4 * r + 4, :],
                        misc_ps[0:PAIR_ROWS, :].rearrange("f (d b) -> f d b", d=4),
                        ACT.Copy).then_inc(x0T_copied, 1)

            def copy_x0r(t, g):
                n = t * GROUPS + g
                act.wait_ge(x0r_turned, n + 1)
                if isinstance(n, int) and n < 2:
                    act.wait_ge(ones_set, 1)
                else:
                    act.wait_ge(vector_scaled, (n - 1) * SLOTS_G * NV)
                    act.wait_ge(spread_made, (n - 1) * SLOTS_G)
                nc.scalar.activation(x0r[:, g % 2, :, 0:FIELDS],
                                     misc_ps[:, 0:SLOTS_G * FIELDS].rearrange("p (j f) -> p j f", f=FIELDS),
                                     ACT.Copy).then_inc(x0r_copied, 1)

            def high_x1(t, g):
                n = t * GROUPS + g
                act.wait_ge(pairs_used, (n + 1) * PAIR_TILES)
                if not (isinstance(n, int) and n < 2):
                    act.wait_ge(unit_made, (n - 1) * SLOTS_G * UNITS)
                nc.scalar.activation(x1h[:, g % 2, :], x1_ps[:], ACT.Copy).then_inc(x1_high, 1)

            def scale_unit(t, i, u):
                slot = t * SLOTS + i
                g, j = divmod(i, SLOTS_G)
                a, b = unit_fields(u)
                act.wait_ge(unit_made, slot * UNITS + u + 1)
                for f in range(a, b):
                    last = nc.scalar.activation(scaled[:, i % 2, f, :],
                                                ring[u % RING][:, (f - a) * CROSS:(f - a + 1) * CROSS],
                                                ACT.Copy, scale=x0r[:, g % 2, j, f:f + 1])
                last.then_inc(scalar_scaled, 1)

            def copy_gram(t, i):
                slot = t * SLOTS + i
                act.wait_ge(gram_made, slot + 1)
                if i == 0 and not (isinstance(t, int) and t == 0):
                    act.wait_ge(s3_copied, 2 * t)
                nc.scalar.activation(gram[:, :, i * SLOT_B:(i + 1) * SLOT_B],
                                     gram_ps[:, 0:(FIELDS + 1) * SLOT_B].rearrange("p (f b) -> p f b", b=SLOT_B),
                                     ACT.Copy).then_inc(gram_copied, 1)

            copy_x0T(0)
            copy_x0r(0, 0)
            high_x1(0, 0)

            def body(t, first, last):
                for i in range(SLOTS):
                    g, j = divmod(i, SLOTS_G)
                    more = g + 1 < GROUPS or not last
                    tn, gn = (t, g + 1) if g + 1 < GROUPS else (t + 1, 0)
                    if j == 0:
                        act.wait_ge(x0r_copied, t * GROUPS + g + 1)
                    if not (first and i < 2):
                        act.wait_ge(x2_summed, (t * SLOTS + i - 1) * 2)
                    before = (t, i - LAG - 1) if i > LAG else (t - 1, i - LAG - 1 + SLOTS)
                    for u in SCALAR_UNITS:
                        scale_unit(t, i, u)
                        if more and j == 0 and gn == 0 and u in EMB_COPY_AFTER:
                            copy_x0T(tn, [EMB_COPY_AFTER.index(u)])
                        if more and j == 1 and u == 1:
                            copy_x0r(tn, gn)
                        if (i > LAG or not first) and u == (0 if i == LAG else 6):
                            copy_gram(*before)
                        if more and j == SLOTS_G - 1 and u == 7:
                            high_x1(tn, gn)

            tiles(act, body)
            for i in range(SLOTS - LAG - 1, SLOTS):
                copy_gram(TILES - 1, i)
            for h in range(2):
                cols = slice(512 * h, 512 * h + 512)
                for k in range(HID1 // 128):
                    act.wait_ge(hid1_made, 4 * h + k + 1)
                    if h == 0 and k == 0:
                        act.wait_ge(tower_in, 7 * 16)
                        act.wait_ge(x2_summed, 2 * TILES * SLOTS)
                    nc.scalar.activation(hid1[:, k, cols], ring[k][:], ACT.Relu, bias=BT1[:, k:k + 1]
                                         ).then_inc(hid1_copied, 1)
                for k in range(HID2 // 128):
                    act.wait_ge(hid2_made, 2 * h + k + 1)
                    nc.scalar.activation(hid2[:, k, cols], (x1_ps, gram_ps)[k][:], ACT.Relu, bias=BT2[:, k:k + 1]
                                         ).then_inc(hid2_copied, 1)
                act.wait_ge(y_made, h + 1)
                nc.scalar.activation(y_row[:, cols], misc_ps[0:1, :], ACT.Copy).then_inc(y_copied, 1)

        @block.vector
        def _(dve):
            nc.vector.memset(x0r[:, :, :, FIELDS:FIELDS + 1], 1.0).then_inc(ones_set, 1)
            dve.wait_ge(weights_in, 64)
            nc.vector.tensor_tensor(W0[:], W0[:], shifted[0:PAIR_ROWS, 1, :, 0:CROSS], ALU.add).then_inc(w0_summed, 1)
            dve.wait_ge(w1_high, 1)
            nc.vector.tensor_tensor(W1l[:], W2[:].rearrange("p f m -> p (f m)"), W1h[:].bitcast(F32),
                                    ALU.subtract).then_inc(w1_low, 1)

            def make_pairs(t, g, ks):
                n = t * GROUPS + g
                for k in ks:
                    c = g * PAIR_TILES + k
                    rows = pair_rows(k)
                    if k == 0:
                        dve.wait_ge(x0T_copied, (t + 1) * 4)
                        dve.wait_ge(shifted_in[g % 2], (t * (GROUPS // 2) + g // 2 + 1) * SHIFTS * 16)
                    if not (isinstance(t, int) and t == 0 and c < PAIR_RING):
                        dve.wait_ge(pairs_used, t * GROUPS * PAIR_TILES + c - PAIR_RING + 1)
                    nc.vector.tensor_tensor(pairs[0:rows, c % PAIR_RING, :], shifted[0:rows, g % 2, k, :],
                                            x0T[0:rows, g * GROUP_COLS:(g + 1) * GROUP_COLS],
                                            ALU.mult).then_inc(pairs_made, 1)

            def low_x1(t, g):
                n = t * GROUPS + g
                dve.wait_ge(pairs_used, (n + 1) * PAIR_TILES)
                dve.wait_ge(x1_high, n + 1)
                nb = GROUP_COLS // DIM
                nc.vector.tensor_reduce(S[:, 0, bass.ds(n * nb, nb)],
                                        x1_ps[:].rearrange("p (b d) -> p b d", d=DIM), AX.X, ALU.add
                                        ).then_inc(x1_low, 1)
                nc.vector.tensor_tensor(x1l[:, g % 2, :], x1_ps[:], x1h[:, g % 2, :].bitcast(F32),
                                        ALU.subtract).then_inc(x1_low, 1)

            def scale_unit(t, i, u):
                slot = t * SLOTS + i
                g, j = divmod(i, SLOTS_G)
                a, b = unit_fields(u)
                if u == VECTOR_UNITS[0] and not (isinstance(slot, int) and slot < 2):
                    dve.wait_ge(x2_summed, 2 * (slot - 1))
                dve.wait_ge(unit_made, slot * UNITS + u + 1)
                nc.vector.tensor_tensor(scaled[:, i % 2, a:b, :],
                                        ring[u % RING][:, 0:(b - a) * CROSS].rearrange("p (f m) -> p f m", m=CROSS),
                                        x0r[:, g % 2, j, a:b].unsqueeze(2).to_broadcast([128, b - a, CROSS]),
                                        ALU.mult).then_inc(vector_scaled, 1)

            def sum_x2(t, i, half):
                slot = t * SLOTS + i
                if half == 0:
                    dve.wait_ge(scalar_scaled, (slot + 1) * NS)
                    dve.wait_ge(vector_scaled, (slot + 1) * NV)
                    if not isinstance(slot, int) or slot >= X2_RING:
                        dve.wait_ge(gram_made, slot - X2_RING + 1)
                cols = slice(64 * half, 64 * half + 64)
                nc.vector.tensor_reduce(x2[:, i % X2_RING, cols],
                                        scaled[:, i % 2, :, cols].rearrange("p f m -> p m f"), AX.X, ALU.add
                                        ).then_inc(x2_summed, 1)

            def copy_s3(t):
                dve.wait_ge(s3_made, t + 1)
                cols = bass.ds(t * TILE_B, TILE_B)
                nc.vector.tensor_copy(S[:, 2, cols], misc_ps[:, 0:TILE_B]).then_inc(s3_copied, 1)
                nc.vector.tensor_copy(S[:, 1, cols], gram[:, FIELDS, :]).then_inc(s3_copied, 1)

            make_pairs(0, 0, range(PAIR_TILES))
            low_x1(0, 0)

            def body(t, first, last):
                for i in range(SLOTS):
                    g, j = divmod(i, SLOTS_G)
                    more = g + 1 < GROUPS or not last
                    tn, gn = (t, g + 1) if g + 1 < GROUPS else (t + 1, 0)
                    if j == 0:
                        dve.wait_ge(x0r_copied, t * GROUPS + g + 1)
                    before = not (first and i == 0)
                    tb, ib = (t, i - 1) if i else (t - 1, SLOTS - 1)
                    scale_unit(t, i, 2)
                    if more and j == 3:
                        make_pairs(tn, gn, range(4, 6))
                    if before:
                        sum_x2(tb, ib, 0)
                    if more and j == 3:
                        make_pairs(tn, gn, range(6, PAIR_TILES))
                    if more and j == 2:
                        make_pairs(tn, gn, range(0, 2))
                    scale_unit(t, i, 5)
                    if i == LAG + 1 and not first:
                        copy_s3(t - 1)
                    if before:
                        sum_x2(tb, ib, 1)
                    if more and j == 2:
                        make_pairs(tn, gn, range(2, 4))
                    scale_unit(t, i, 8)
                    if more and j == 3:
                        low_x1(tn, gn)

            tiles(dve, body)
            sum_x2(TILES - 1, SLOTS - 1, 0)
            sum_x2(TILES - 1, SLOTS - 1, 1)
            copy_s3(TILES - 1)

        @block.tensor
        def _(pe):
            def turn_emb(t, rounds=range(4)):
                by_dim = emb[:].rearrange("p (f d) -> p d f", d=DIM)
                for r in rounds:
                    if r == 0:
                        pe.wait_ge(emb_copied, (t + 1) * (PER_TILE - 1))
                        if not isinstance(t, int) or t > 0:
                            pe.wait_ge(x0r_copied, t * GROUPS)
                    else:
                        pe.wait_ge(x0T_copied, t * 4 + r)
                    for q in range(4):
                        mm = nc.tensor.transpose(misc_ps[0:PAIR_ROWS, q * TILE_B:(q + 1) * TILE_B],
                                                 by_dim[:, 4 * r + q, :], eye[:])
                    mm.then_inc(emb_turned, 1)

            def before_x0r(t, g):
                n = t * GROUPS + g
                if g == 0:
                    pe.wait_ge(x0T_copied, (t + 1) * 4)
                else:
                    pe.wait_ge(x0r_copied, n)
                    if g == 2 and not (isinstance(t, int) and t == 0):
                        pe.wait_ge(s3_copied, 2 * t)

            def turn_x0r(g):
                for j in range(SLOTS_G):
                    c = g * GROUP_COLS + j * ROWS
                    mm = nc.tensor.transpose(misc_ps[:, j * FIELDS:(j + 1) * FIELDS],
                                             x0T[0:FIELDS, c:c + ROWS], eye[0:FIELDS, 0:FIELDS])
                mm.then_inc(x0r_turned, 1)

            def first_layer(t, g, ks=range(PAIR_TILES)):
                n = t * GROUPS + g
                if ks[0] == 0 and not (isinstance(n, int) and n == 0):
                    pe.wait_ge(x1_low, 2 * n)
                for k in ks:
                    rows = pair_rows(k)
                    pe.wait_ge(pairs_made, n * PAIR_TILES + k + 1)
                    nc.tensor.matmul(x1_ps[:], W0[0:rows, k, :], pairs[0:rows, (g * PAIR_TILES + k) % PAIR_RING, :],
                                     start=(k == 0), stop=(k == PAIR_TILES - 1)).then_inc(pairs_used, 1)

            def unit(t, i, u):
                slot = t * SLOTS + i
                g, j = divmod(i, SLOTS_G)
                a, b = unit_fields(u)
                if u >= RING:
                    pe.wait_ge(*scaled_before(u - RING, slot))
                elif not (isinstance(slot, int) and slot == 0):
                    pe.wait_ge(*scaled_before(u + UNITS - RING, slot - 1))
                w = slice(a * CROSS, b * CROSS)
                c = slice(j * ROWS, (j + 1) * ROWS)
                dst = ring[u % RING][:, 0:(b - a) * CROSS]
                nc.tensor.matmul(dst, x1h[:, g % 2, c], W1h[:, w], start=True, stop=False)
                nc.tensor.matmul(dst, x1h[:, g % 2, c], W1l[:, w], start=False, stop=False)
                nc.tensor.matmul(dst, x1l[:, g % 2, c], W1h[:, w], start=False, stop=True).then_inc(unit_made, 1)

            def gram_slot(t, i):
                slot = t * SLOTS + i
                pe.wait_ge(x2_summed, 2 * (slot + 1))
                pe.wait_ge(spread_made, slot + 1)
                if not isinstance(slot, int) or slot > 0:
                    pe.wait_ge(gram_copied, slot)
                nc.tensor.matmul(gram_ps[:, 0:(FIELDS + 1) * SLOT_B], x2[:, i % X2_RING, :],
                                 spread[:, i % X2_RING, :, :].rearrange("p f b -> p (f b)"),
                                 start=True, stop=True).then_inc(gram_made, 1)

            def third_layer(t, fields):
                if fields[0] == 0:
                    pe.wait_ge(gram_copied, (t + 1) * SLOTS)
                    pe.wait_ge(w1_in, 32)
                    if isinstance(t, int) and t == TILES - 1:
                        pe.wait_ge(x0r_copied, TILES * GROUPS)
                        pe.wait_ge(s3_copied, 2 * t)
                    else:
                        pe.wait_ge(x0r_copied, (t + 1) * GROUPS + 2)
                for f in fields:
                    mm = nc.tensor.matmul(misc_ps[:, 0:TILE_B], W2[:, f, :], gram[:, f, :],
                                          start=(f == 0), stop=(f == FIELDS - 1))
                if fields[-1] == FIELDS - 1:
                    mm.then_inc(s3_made, 1)

            pe.wait_ge(weights_in, 64)
            turn_emb(0)
            before_x0r(0, 0)
            turn_x0r(0)
            pe.wait_ge(w0_summed, 1)
            first_layer(0, 0)

            def body(t, first, last):
                for i in range(SLOTS):
                    g, j = divmod(i, SLOTS_G)
                    more = g + 1 < GROUPS or not last
                    tn, gn = (t, g + 1) if g + 1 < GROUPS else (t + 1, 0)
                    if j == 0:
                        pe.wait_ge(x1_high, t * GROUPS + g + 1)
                        pe.wait_ge(x1_low, 2 * (t * GROUPS + g + 1))
                    if first and i == 0:
                        pe.wait_ge(w1_low, 1)
                    if more and j == 1:
                        before_x0r(tn, gn)
                    for u in range(UNITS):
                        unit(t, i, u)
                        if more and j == 1 and u == 0:
                            turn_x0r(gn)
                        if more and j == 0 and gn == 0 and u in EMB_TURN_AFTER:
                            turn_emb(tn, [EMB_TURN_AFTER.index(u)])
                        if more and j == SLOTS_G - 1 and 1 <= u <= PAIR_TILES:
                            first_layer(tn, gn, [u - 1])
                        place = (i - LAG) * UNITS + u - 1
                        if not first and 0 <= 4 * place < FIELDS:
                            third_layer(t - 1, range(4 * place, min(4 * place + 4, FIELDS)))
                    if i >= LAG:
                        gram_slot(t, i - LAG)
                    elif not first:
                        gram_slot(t - 1, i - LAG + SLOTS)

            tiles(pe, body)
            for i in range(SLOTS - LAG, SLOTS):
                gram_slot(TILES - 1, i)
            third_layer(TILES - 1, range(FIELDS))

            pe.wait_ge(tower_in, 7 * 16)
            pe.wait_ge(s3_copied, 2 * TILES)
            pe.wait_ge(scalar_scaled, TILES * SLOTS * NS)
            pe.wait_ge(vector_scaled, TILES * SLOTS * NV)
            pe.wait_ge(gram_copied, TILES * SLOTS)
            for h in range(2):
                cols = slice(512 * h, 512 * h + 512)
                for k in range(HID1 // 128):
                    rows = slice(128 * k, 128 * k + 128)
                    if h > 0:
                        pe.wait_ge(hid1_copied, k + 1)
                    for c in range(3):
                        nc.tensor.matmul(ring[k][:], WT1[:, c, rows], S[:, c, cols], start=(c == 0), stop=False)
                    nc.tensor.matmul(ring[k][:], WT1d[:, rows], denseT[:, cols], start=False, stop=True
                                     ).then_inc(hid1_made, 1)
                pe.wait_ge(hid1_copied, 4 * h + 4)
                for k in range(HID2 // 128):
                    if h > 0:
                        pe.wait_ge(hid2_copied, k + 1)
                    for c in range(HID1 // 128):
                        mm = nc.tensor.matmul((x1_ps, gram_ps)[k][:], WT2[:, c, 128 * k:128 * k + 128],
                                              hid1[:, c, cols], start=(c == 0), stop=(c == HID1 // 128 - 1))
                    mm.then_inc(hid2_made, 1)
                pe.wait_ge(hid2_copied, 2 * h + 2)
                if h > 0:
                    pe.wait_ge(y_copied, h)
                for c in range(HID2 // 128):
                    mm = nc.tensor.matmul(misc_ps[0:1, :], WT3[:, c:c + 1], hid2[:, c, cols],
                                          start=(c == 0), stop=(c == HID2 // 128 - 1))
                mm.then_inc(y_made, 1)


def kernel(**inputs):
    import numpy as np
    import concourse.bacc as bacc
    from concourse.bass_utils import run_bass_kernel_spmd

    a = {k: np.asarray(v) for k, v in inputs.items()}
    g = np.arange(FIELDS)
    one = np.concatenate([g * FIELDS + (g + s) % FIELDS for s in range(SHIFTS)])
    other = np.concatenate([(g + s) % FIELDS * FIELDS + g for s in range(SHIFTS)])
    f0 = a["L0_rec_f0"]
    w0 = np.zeros((2, PAIR_TILES * PAIR_ROWS, CROSS), f0.dtype)
    w0[0, :SHIFTS * FIELDS] = f0[one]
    w0[1, FIELDS:SHIFTS * FIELDS] = f0[other[FIELDS:]]
    w0 = w0.reshape(2, PAIR_TILES, PAIR_ROWS, CROSS).transpose(0, 2, 1, 3)

    def by_partition(x, width):
        return x.reshape(-1, 128, width).transpose(1, 0, 2)

    arrays = {
        "ids": a["ids"].reshape(TILES, TILE_B, FIELDS).transpose(1, 0, 2),
        "ident": np.eye(128, dtype=np.float32),
        "block_mask": np.kron(np.eye(SLOT_B, dtype=np.float32), np.ones((DIM, 1), np.float32)),
        "w0a": w0[0], "w0b": w0[1],
        "w1": a["L0_rec_f1"].reshape(FIELDS, CROSS, CROSS).transpose(1, 0, 2),
        "w2": a["L0_rec_f2"].reshape(FIELDS, CROSS, CROSS).transpose(1, 0, 2),
        "dense_t": a["dense_ctx"].T,
        "wt1": by_partition(a["W_top1"][:3 * CROSS], HID1),
        "wt1d": a["W_top1"][3 * CROSS:],
        "bt1": a["b_top1"].reshape(-1, 128).T,
        "wt2": by_partition(a["W_top2"], HID2),
        "bt2": a["b_top2"].reshape(-1, 128).T,
        "wt3": a["W_top3"].reshape(-1, 128).T,
    }
    arrays |= {f"tbl_{f}": a[f"tbl_{f}"] for f in range(FIELDS)}
    arrays = {f"in_{k}": np.ascontiguousarray(v) for k, v in arrays.items()}
    nc = bacc.Bacc("TRN2", target_bir_lowering=False, num_devices=1)
    aps = {k[3:]: nc.dram_tensor(k, v.shape, mybir.dt.from_np(v.dtype), kind="ExternalInput").ap()
           for k, v in arrays.items()}
    tables = [aps.pop(f"tbl_{f}") for f in range(FIELDS)]
    out = nc.dram_tensor("out_y", (1, BATCH), F32, kind="ExternalOutput").ap()
    cin_tower(nc, tables=tables, out=out, **aps)
    r = run_bass_kernel_spmd(nc, [arrays], core_ids=[0])
    return r.results[0]["out_y"].reshape(BATCH, 1)
```

```python
import concourse.bass as bass
from concourse import mybir
from contextlib import ExitStack

F32 = mybir.dt.float32
F32R = mybir.dt.float32r
I32 = mybir.dt.int32
ALU = mybir.AluOpType
ACT = mybir.ActivationFunctionType
AX = mybir.AxisListType

BATCH = 1024
FIELDS = 39
DIM = 16
CROSS = 128
DENSE = 16
HID1 = 512
HID2 = 256

TILE_B = 128
TILES = BATCH // TILE_B
TILE_COLS = TILE_B * DIM
GROUP_COLS = 512
GROUPS = TILE_COLS // GROUP_COLS
ROWS = 128
SLOTS = TILE_COLS // ROWS
SLOTS_G = SLOTS // GROUPS
SLOT_B = ROWS // DIM

SHIFTS = (FIELDS + 1) // 2
PER_TILE = 3
PAIR_TILES = -(-SHIFTS // PER_TILE)
PAIR_ROWS = PER_TILE * FIELDS
TURNED_ROWS = PAIR_ROWS + PAIR_TILES - 1
SHIFT_DMAS = PER_TILE + PAIR_TILES - 1

UNITS = -(-FIELDS // 4)
RING = 5
VECTOR_UNITS = (2, 5, 8)
SCALAR_UNITS = tuple(u for u in range(UNITS) if u not in VECTOR_UNITS)
EMB_TURN_AFTER = (0, 3, 6, 9)
EMB_COPY_AFTER = (1, 4, 7, 9)
LAG = 2
PAIR_RING = 5
X2_RING = 4


PLACE = {0: 0, 1: 4, 6: 8, 2: 12, 5: 16, 8: 20, 9: 24, 3: 27, 4: 31, 7: 35}
KEPT = 27
HEAD = 9
FOLDS = ((4, 27, 0, 8), (7, 35, 8, 4))


def unit_fields(u):
    return 4 * u, min(4 * u + 4, FIELDS)


def pair_rows(k):
    return len(range(k, SHIFTS, PAIR_TILES)) * FIELDS


def cin_tower(nc, ids, tables, ident, block_mask, w0a, w0b, w1, w2, dense_t, wt1, wt1d, bt1, wt2, bt2, wt3, out):
    with ExitStack() as ctx:
        def sb(name, shape, dt=F32):
            return ctx.enter_context(nc.sbuf_tensor(name, shape, dt))

        def bank(name):
            return ctx.enter_context(nc.psum_tensor(name, [128, 512], F32))

        def sem(name):
            return ctx.enter_context(nc.semaphore(name))

        eye = sb("eye", [128, 128])
        mask = sb("mask", [128, SLOT_B])
        W0 = sb("W0", [PAIR_ROWS, PAIR_TILES, CROSS])
        W1h = sb("W1h", [128, FIELDS * CROSS], F32R)
        W1l = sb("W1l", [128, FIELDS * CROSS], F32R)
        W2 = sb("W2", [128, FIELDS, CROSS])
        BT1 = sb("BT1", [128, HID1 // 128])
        BT2 = sb("BT2", [128, HID2 // 128])
        WT3 = sb("WT3", [128, HID2 // 128])
        idx = sb("idx", [128, FIELDS], I32)
        emb = sb("emb", [128, TURNED_ROWS * DIM])
        x0T = sb("x0T", [TURNED_ROWS, TILE_COLS])
        shifted = sb("shifted", [128, 2, PAIR_TILES, GROUP_COLS])
        pairs = sb("pairs", [PAIR_ROWS, PAIR_RING, GROUP_COLS])
        x0r = sb("x0r", [128, 2, SLOTS_G, FIELDS + 1])
        x1h = sb("x1h", [128, 2, GROUP_COLS], F32R)
        x1l = sb("x1l", [128, 2, GROUP_COLS], F32R)
        scaled = sb("scaled", [128, 2, FIELDS, CROSS])
        x2 = sb("x2", [128, X2_RING, CROSS])
        spread = sb("spread", [128, X2_RING, FIELDS + 1, SLOT_B])
        gram = sb("gram", [128, FIELDS + 1, TILE_B])
        S = sb("S", [128, 3, BATCH])

        tower = shifted[:].rearrange("p a k c -> p (a k) c")
        WT1 = tower[:, 0:3, :]
        WT1d = tower[0:DENSE, 3, :]
        WT2 = tower[:, 4:6, :].rearrange("p k (c m) -> p (k c) m", m=HID2)
        denseT = tower[0:DENSE, 6:8, :].rearrange("p a b -> p (a b)")
        hid1 = scaled[:, 0, 0:HID1 // 128 * 8, :].rearrange("p (k c) m -> p k (c m)", k=HID1 // 128)
        hid2 = scaled[:, 1, 0:HID2 // 128 * 8, :].rearrange("p (k c) m -> p k (c m)", k=HID2 // 128)
        y_row = pairs[0:1, 0:2, :].rearrange("p a b -> p (a b)")

        ring = [bank(f"ring{i}") for i in range(RING)]
        x1_ps = bank("x1_ps")
        misc_ps = bank("misc_ps")
        gram_ps = bank("gram_ps")

        weights_in = sem("weights_in")
        tower_in = sem("tower_in")
        w1_in = sem("w1_in")
        w1_high = sem("w1_high")
        w1_low = sem("w1_low")
        w0_summed = sem("w0_summed")
        ones_set = sem("ones_set")
        idx_in = sem("idx_in")
        gathered = sem("gathered")
        emb_copied = sem("emb_copied")
        emb_turned = sem("emb_turned")
        x0T_copied = sem("x0T_copied")
        shifted_in = [sem("shifted_in0"), sem("shifted_in1")]
        x0r_turned = sem("x0r_turned")
        x0r_copied = sem("x0r_copied")
        pairs_made = sem("pairs_made")
        pairs_used = sem("pairs_used")
        x1_high = sem("x1_high")
        x1_low = sem("x1_low")
        unit_made = sem("unit_made")
        scalar_scaled = sem("scalar_scaled")
        vector_scaled = sem("vector_scaled")
        x2_summed = sem("x2_summed")
        folded = sem("folded")
        spread_made = sem("spread_made")
        gram_made = sem("gram_made")
        gram_copied = sem("gram_copied")
        s3_made = sem("s3_made")
        s3_copied = sem("s3_copied")
        hid1_made = sem("hid1_made")
        hid1_copied = sem("hid1_copied")
        hid2_made = sem("hid2_made")
        hid2_copied = sem("hid2_copied")
        y_made = sem("y_made")
        y_copied = sem("y_copied")
        y_out = sem("y_out")

        NS = len(SCALAR_UNITS)
        NV = len(VECTOR_UNITS)

        def scaled_before(u, slot):
            if u in VECTOR_UNITS:
                return vector_scaled, slot * NV + VECTOR_UNITS.index(u) + 1
            return scalar_scaled, slot * NS + SCALAR_UNITS.index(u) + 1

        E = FIELDS * DIM
        copies = ((emb[:, E:3 * E].rearrange("p (c e) -> p c e", e=E), emb[:, 0:E].unsqueeze(1).to_broadcast([128, 2, E])),
                  (emb[:, 3 * E:TURNED_ROWS * DIM], emb[:, 0:TURNED_ROWS * DIM - 3 * E]))

        def copy_x0T_round(r, bank):
            return (x0T[:].rearrange("f (b d) -> f d b", d=DIM)[:, 4 * r:4 * r + 4, :],
                    bank[0:TURNED_ROWS, :].rearrange("f (d b) -> f d b", d=4))

        def tiles(eng, body):
            body(0, True, 2)
            with eng.Fori(1, TILES - 2) as t:
                body(t, False, 2)
            body(TILES - 2, False, 1)
            body(TILES - 1, False, 0)

        block = ctx.enter_context(nc.Block())

        @block.sync
        def _(sp):
            sp.dma_start(eye[:], ident).then_inc(weights_in, 16)
            sp.dma_start(mask[:], block_mask).then_inc(weights_in, 16)
            sp.dma_start(W0[:], w0a).then_inc(weights_in, 16)
            sp.dma_start(shifted[0:PAIR_ROWS, 1, :, 0:CROSS], w0b).then_inc(weights_in, 16)
            sp.dma_start(W2[:], w1).then_inc(w1_in, 16)

            def shift_group(t, g):
                n = t * GROUPS + g
                p = g % 2
                if g == 0:
                    sp.wait_ge(x0T_copied, (t + 1) * 4)
                elif not (isinstance(n, int) and n < 2):
                    sp.wait_ge(pairs_made, (n - 1) * PAIR_TILES)
                else:
                    sp.wait_ge(w0_summed, 1)
                cols = slice(g * GROUP_COLS, (g + 1) * GROUP_COLS)
                for i in range(PER_TILE):
                    start = -PAIR_TILES * i % FIELDS
                    sp.dma_start(shifted[i * FIELDS:(i + 1) * FIELDS, p, 0, :], x0T[start:start + FIELDS, cols]
                                 ).then_inc(shifted_in[p], 16)
                for k in range(1, PAIR_TILES):
                    sp.dma_start(shifted[0:pair_rows(k), p, k, :], x0T[k:k + pair_rows(k), cols]
                                 ).then_inc(shifted_in[p], 16)

            def body(t, first, left):
                for g in range(GROUPS):
                    shift_group(t, g)
                    if first and g == 0:
                        sp.wait_ge(w1_low, 1)
                        sp.dma_start(W2[:], w2).then_inc(w1_in, 16)

            tiles(sp, body)
            sp.wait_ge(pairs_made, TILES * GROUPS * PAIR_TILES)
            for dst, src in ((WT1, wt1), (WT1d, wt1d), (BT1[:], bt1), (WT2, wt2), (BT2[:], bt2), (WT3[:], wt3),
                             (denseT, dense_t)):
                sp.dma_start(dst, src).then_inc(tower_in, 16)
            sp.wait_ge(y_copied, 2)
            sp.dma_start(out, y_row).then_inc(y_out, 16)
            sp.wait_ge(y_out, 16)

        @block.gpsimd
        def _(pool):
            def load_idx(t):
                if not isinstance(t, int) or t > 0:
                    pool.wait_ge(gathered, t * FIELDS * 16)
                pool.dma_start(idx[:], ids[:, bass.ds(t, 1), :].rearrange("p t f -> p (t f)")
                               if not isinstance(t, int) else ids[:, t, :]).then_inc(idx_in, 16)

            def idx_loaded(t):
                pool.wait_ge(idx_in, (t + 1) * 16)

            def rows_gathered(t):
                pool.wait_ge(gathered, (t + 1) * FIELDS * 16)

            def gather(t, fields):
                for f in fields:
                    pool.indirect_dma_start(
                        emb[:, f * DIM:(f + 1) * DIM], None, tables[f],
                        bass.IndirectOffsetOnAxis(ap=idx[:, f:f + 1], axis=0)).then_inc(gathered, 16)

            def triple(t):
                for copy in (copies[0], copies[1]):
                    pool.tensor_copy(*copy).then_inc(emb_copied, 1)

            def make_spread(t, i):
                slot = t * SLOTS + i
                g, j = divmod(i, SLOTS_G)
                if j == 0:
                    pool.wait_ge(x0r_copied, t * GROUPS + g + 1)
                if not isinstance(slot, int) or slot >= X2_RING:
                    pool.wait_ge(gram_made, slot - X2_RING + 1)
                pool.tensor_tensor(
                    spread[:, i % X2_RING, :, :],
                    x0r[:, g % 2, j, :].unsqueeze(2).to_broadcast([128, FIELDS + 1, SLOT_B]),
                    mask[:].unsqueeze(1).to_broadcast([128, FIELDS + 1, SLOT_B]),
                    ALU.mult).then_inc(spread_made, 1)

            def fold(t, i, n):
                unit, source, onto, k = FOLDS[n]
                slot = t * SLOTS + i
                pool.wait_ge(scalar_scaled, slot * NS + SCALAR_UNITS.index(unit) + 1)
                pool.tensor_tensor(scaled[:, i % 2, onto:onto + k, :], scaled[:, i % 2, onto:onto + k, :],
                                   scaled[:, i % 2, source:source + k, :], ALU.add).then_inc(folded, 1)

            load_idx(0)
            idx_loaded(0)
            gather(0, range(FIELDS))
            pool.wait_ge(emb_turned, 4)
            load_idx(1)
            pool.wait_ge(weights_in, 64)
            pool.wait_ge(ones_set, 1)

            def body(t, first, left):
                for i in range(SLOTS):
                    if i == 0 and left and first:
                        idx_loaded(t + 1)
                    if i == 10 and left:
                        rows_gathered(t + 1)
                    if i == 13 and left > 1:
                        idx_loaded(t + 2)
                    make_spread(t, i)
                    if i < 10 and left:
                        if i == 0 and first:
                            gather(t + 1, range(HEAD))
                        gather(t + 1, range(HEAD + 3 * i, HEAD + 3 * i + 3))
                    fold(t, i, 0)
                    if i == 10 and left:
                        triple(t + 1)
                    fold(t, i, 1)
                    if i == 12 and left > 1:
                        pool.wait_ge(emb_turned, (t + 2) * 4)
                        load_idx(t + 2)
                    if i >= 13 and left > 1:
                        gather(t + 2, range(3 * i - 39, 3 * i - 36))

            tiles(pool, body)

        @block.scalar
        def _(act):
            act.wait_ge(w1_in, 16)
            nc.scalar.activation(W1h[:], W2[:].rearrange("p f m -> p (f m)"), ACT.Copy).then_inc(w1_high, 1)

            def copy_x0T(t, rounds=range(4)):
                for r in rounds:
                    act.wait_ge(emb_turned, t * 4 + r + 1)
                    if r == 0:
                        act.wait_ge(pairs_made, t * GROUPS * PAIR_TILES)
                        act.wait_ge(x0r_turned, t * GROUPS)
                    nc.scalar.activation(*copy_x0T_round(r, misc_ps), ACT.Copy).then_inc(x0T_copied, 1)

            def copy_x0r(t, g):
                n = t * GROUPS + g
                act.wait_ge(x0r_turned, n + 1)
                if isinstance(n, int) and n < 2:
                    act.wait_ge(ones_set, 1)
                else:
                    act.wait_ge(vector_scaled, (n - 1) * SLOTS_G * NV)
                    act.wait_ge(spread_made, (n - 1) * SLOTS_G)
                nc.scalar.activation(x0r[:, g % 2, :, 0:FIELDS],
                                     misc_ps[:, 0:SLOTS_G * FIELDS].rearrange("p (j f) -> p j f", f=FIELDS),
                                     ACT.Copy).then_inc(x0r_copied, 1)

            def high_x1(t, g):
                n = t * GROUPS + g
                act.wait_ge(pairs_used, (n + 1) * PAIR_TILES)
                if not (isinstance(n, int) and n < 2):
                    act.wait_ge(unit_made, (n - 1) * SLOTS_G * UNITS)
                nc.scalar.activation(x1h[:, g % 2, :], x1_ps[:], ACT.Copy).then_inc(x1_high, 1)

            def scale_unit(t, i, u):
                slot = t * SLOTS + i
                g, j = divmod(i, SLOTS_G)
                a, b = unit_fields(u)
                act.wait_ge(unit_made, slot * UNITS + u + 1)
                for f in range(a, b):
                    last = nc.scalar.activation(scaled[:, i % 2, PLACE[u] + f - a, :],
                                                ring[u % RING][:, (f - a) * CROSS:(f - a + 1) * CROSS],
                                                ACT.Copy, scale=x0r[:, g % 2, j, f:f + 1])
                last.then_inc(scalar_scaled, 1)

            def copy_gram(t, i):
                slot = t * SLOTS + i
                act.wait_ge(gram_made, slot + 1)
                if i == 0 and not (isinstance(t, int) and t == 0):
                    act.wait_ge(s3_copied, 2 * t)
                nc.scalar.activation(gram[:, :, i * SLOT_B:(i + 1) * SLOT_B],
                                     gram_ps[:, 0:(FIELDS + 1) * SLOT_B].rearrange("p (f b) -> p f b", b=SLOT_B),
                                     ACT.Copy).then_inc(gram_copied, 1)

            act.wait_ge(gathered, FIELDS * 16)
            nc.scalar.activation(*copies[1], ACT.Copy).then_inc(emb_copied, 1)
            for r in (0, 2):
                act.wait_ge(emb_turned, r + 1)
                nc.scalar.activation(*copy_x0T_round(r, ring[r]), ACT.Copy).then_inc(x0T_copied, 1)
            copy_x0r(0, 0)
            high_x1(0, 0)

            def body(t, first, left):
                for i in range(SLOTS):
                    g, j = divmod(i, SLOTS_G)
                    more = g + 1 < GROUPS or left > 0
                    tn, gn = (t, g + 1) if g + 1 < GROUPS else (t + 1, 0)
                    if j == 0:
                        act.wait_ge(x0r_copied, t * GROUPS + g + 1)
                    if not (first and i < 2):
                        act.wait_ge(x2_summed, (t * SLOTS + i - 1) * 2)
                    before = (t, i - LAG - 1) if i > LAG else (t - 1, i - LAG - 1 + SLOTS)
                    for u in SCALAR_UNITS:
                        scale_unit(t, i, u)
                        if more and j == 0 and gn == 0 and u in EMB_COPY_AFTER:
                            copy_x0T(tn, [EMB_COPY_AFTER.index(u)])
                        if more and j == 1 and u == 4:
                            copy_x0r(tn, gn)
                        if (i > LAG or not first) and u == (6 if i == LAG + 1 else 0):
                            copy_gram(*before)
                        if more and j == SLOTS_G - 1 and u == 6:
                            high_x1(tn, gn)

            tiles(act, body)
            for i in range(SLOTS - LAG - 1, SLOTS):
                copy_gram(TILES - 1, i)
            for h in range(2):
                cols = slice(512 * h, 512 * h + 512)
                for k in range(HID1 // 128):
                    act.wait_ge(hid1_made, 4 * h + k + 1)
                    if h == 0 and k == 0:
                        act.wait_ge(tower_in, 7 * 16)
                        act.wait_ge(x2_summed, 2 * TILES * SLOTS)
                    nc.scalar.activation(hid1[:, k, cols], ring[k][:], ACT.Relu, bias=BT1[:, k:k + 1]
                                         ).then_inc(hid1_copied, 1)
                for k in range(HID2 // 128):
                    act.wait_ge(hid2_made, 2 * h + k + 1)
                    nc.scalar.activation(hid2[:, k, cols], (x1_ps, gram_ps)[k][:], ACT.Relu, bias=BT2[:, k:k + 1]
                                         ).then_inc(hid2_copied, 1)
                act.wait_ge(y_made, h + 1)
                nc.scalar.activation(y_row[:, cols], misc_ps[0:1, :], ACT.Copy).then_inc(y_copied, 1)

        @block.vector
        def _(dve):
            nc.vector.memset(x0r[:, :, :, FIELDS:FIELDS + 1], 1.0).then_inc(ones_set, 1)
            dve.wait_ge(weights_in, 64)
            nc.vector.tensor_tensor(W0[:], W0[:], shifted[0:PAIR_ROWS, 1, :, 0:CROSS], ALU.add).then_inc(w0_summed, 1)
            dve.wait_ge(w1_high, 1)
            nc.vector.tensor_tensor(W1l[:], W2[:].rearrange("p f m -> p (f m)"), W1h[:].bitcast(F32),
                                    ALU.subtract).then_inc(w1_low, 1)

            def make_pairs(t, g, ks):
                n = t * GROUPS + g
                for k in ks:
                    rows = pair_rows(k)
                    if k == 0:
                        dve.wait_ge(x0T_copied, (t + 1) * 4)
                        dve.wait_ge(shifted_in[g % 2], (t * (GROUPS // 2) + g // 2 + 1) * SHIFT_DMAS * 16)
                    if k >= PAIR_RING:
                        dve.wait_ge(pairs_used, n * PAIR_TILES + k - PAIR_RING + 1)
                    elif k == 0 and not (isinstance(n, int) and n == 0):
                        dve.wait_ge(pairs_used, n * PAIR_TILES)
                    second = shifted[0:rows, g % 2, k, :] if k else x0T[0:rows, g * GROUP_COLS:(g + 1) * GROUP_COLS]
                    nc.vector.tensor_tensor(pairs[0:rows, k % PAIR_RING, :], shifted[0:rows, g % 2, 0, :], second,
                                            ALU.mult).then_inc(pairs_made, 1)

            def low_x1(t, g):
                n = t * GROUPS + g
                dve.wait_ge(pairs_used, (n + 1) * PAIR_TILES)
                dve.wait_ge(x1_high, n + 1)
                nb = GROUP_COLS // DIM
                nc.vector.tensor_reduce(S[:, 0, bass.ds(n * nb, nb)],
                                        x1_ps[:].rearrange("p (b d) -> p b d", d=DIM), AX.X, ALU.add
                                        ).then_inc(x1_low, 1)
                nc.vector.tensor_tensor(x1l[:, g % 2, :], x1_ps[:], x1h[:, g % 2, :].bitcast(F32),
                                        ALU.subtract).then_inc(x1_low, 1)

            def scale_unit(t, i, u):
                slot = t * SLOTS + i
                g, j = divmod(i, SLOTS_G)
                a, b = unit_fields(u)
                if u == VECTOR_UNITS[0] and not (isinstance(slot, int) and slot < 2):
                    dve.wait_ge(x2_summed, 2 * (slot - 1))
                dve.wait_ge(unit_made, slot * UNITS + u + 1)
                nc.vector.tensor_tensor(scaled[:, i % 2, PLACE[u]:PLACE[u] + b - a, :],
                                        ring[u % RING][:, 0:(b - a) * CROSS].rearrange("p (f m) -> p f m", m=CROSS),
                                        x0r[:, g % 2, j, a:b].unsqueeze(2).to_broadcast([128, b - a, CROSS]),
                                        ALU.mult).then_inc(vector_scaled, 1)

            def sum_x2(t, i, half):
                slot = t * SLOTS + i
                if half == 0:
                    dve.wait_ge(scalar_scaled, (slot + 1) * NS)
                    dve.wait_ge(vector_scaled, (slot + 1) * NV)
                    dve.wait_ge(folded, (slot + 1) * len(FOLDS))
                    if not isinstance(slot, int) or slot >= X2_RING:
                        dve.wait_ge(gram_made, slot - X2_RING + 1)
                cols = slice(64 * half, 64 * half + 64)
                nc.vector.tensor_reduce(x2[:, i % X2_RING, cols],
                                        scaled[:, i % 2, 0:KEPT, cols].rearrange("p f m -> p m f"), AX.X, ALU.add
                                        ).then_inc(x2_summed, 1)

            def copy_s3(t):
                dve.wait_ge(s3_made, t + 1)
                cols = bass.ds(t * TILE_B, TILE_B)
                nc.vector.tensor_copy(S[:, 2, cols], misc_ps[:, 0:TILE_B]).then_inc(s3_copied, 1)
                nc.vector.tensor_copy(S[:, 1, cols], gram[:, FIELDS, :]).then_inc(s3_copied, 1)

            dve.wait_ge(gathered, FIELDS * 16)
            nc.vector.tensor_copy(*copies[0]).then_inc(emb_copied, 1)
            for r in (1, 3):
                dve.wait_ge(emb_turned, r + 1)
                nc.vector.tensor_copy(*copy_x0T_round(r, ring[r])).then_inc(x0T_copied, 1)
            make_pairs(0, 0, range(PAIR_TILES))
            low_x1(0, 0)

            def body(t, first, left):
                for i in range(SLOTS):
                    g, j = divmod(i, SLOTS_G)
                    more = g + 1 < GROUPS or left > 0
                    tn, gn = (t, g + 1) if g + 1 < GROUPS else (t + 1, 0)
                    if j == 0:
                        dve.wait_ge(x0r_copied, t * GROUPS + g + 1)
                    before = not (first and i == 0)
                    tb, ib = (t, i - 1) if i else (t - 1, SLOTS - 1)
                    if more and j == 3:
                        make_pairs(tn, gn, [5])
                    scale_unit(t, i, 2)
                    if i == LAG + 1 and not first:
                        copy_s3(t - 1)
                    if more and j == 3:
                        make_pairs(tn, gn, [6])
                    if before:
                        sum_x2(tb, ib, 0)
                    if more and j == 2:
                        make_pairs(tn, gn, range(0, 2))
                    scale_unit(t, i, 5)
                    if before:
                        sum_x2(tb, ib, 1)
                    if more and j == 2:
                        make_pairs(tn, gn, range(2, 5))
                    if more and j == 3:
                        low_x1(tn, gn)
                    scale_unit(t, i, 8)

            tiles(dve, body)
            sum_x2(TILES - 1, SLOTS - 1, 0)
            sum_x2(TILES - 1, SLOTS - 1, 1)
            copy_s3(TILES - 1)

        @block.tensor
        def _(pe):
            def turn_emb(t, rounds=range(4)):
                by_dim = emb[:].rearrange("p (f d) -> p d f", d=DIM)
                for r in rounds:
                    if r == 0:
                        pe.wait_ge(emb_copied, (t + 1) * len(copies))
                    if isinstance(t, int) and t == 0:
                        bank = ring[r]
                    else:
                        bank = misc_ps
                        if r == 0:
                            pe.wait_ge(x0r_copied, t * GROUPS)
                        else:
                            pe.wait_ge(x0T_copied, t * 4 + r)
                    for q in range(4):
                        mm = nc.tensor.transpose(bank[0:TURNED_ROWS, q * TILE_B:(q + 1) * TILE_B],
                                                 by_dim[:, 4 * r + q, :], eye[:])
                    mm.then_inc(emb_turned, 1)

            def before_x0r(t, g):
                n = t * GROUPS + g
                if g == 0:
                    pe.wait_ge(x0T_copied, (t + 1) * 4)
                else:
                    pe.wait_ge(x0r_copied, n)
                    if g == 2 and not (isinstance(t, int) and t == 0):
                        pe.wait_ge(s3_copied, 2 * t)

            def turn_x0r(g):
                for j in range(SLOTS_G):
                    c = g * GROUP_COLS + j * ROWS
                    mm = nc.tensor.transpose(misc_ps[:, j * FIELDS:(j + 1) * FIELDS],
                                             x0T[0:FIELDS, c:c + ROWS], eye[0:FIELDS, 0:FIELDS])
                mm.then_inc(x0r_turned, 1)

            def first_layer(t, g, ks=range(PAIR_TILES)):
                n = t * GROUPS + g
                if ks[0] == 0 and not (isinstance(n, int) and n == 0):
                    pe.wait_ge(x1_low, 2 * n)
                for k in ks:
                    rows = pair_rows(k)
                    pe.wait_ge(pairs_made, n * PAIR_TILES + k + 1)
                    nc.tensor.matmul(x1_ps[:], W0[0:rows, k, :], pairs[0:rows, k % PAIR_RING, :],
                                     start=(k == 0), stop=(k == PAIR_TILES - 1)).then_inc(pairs_used, 1)

            def unit(t, i, u):
                slot = t * SLOTS + i
                g, j = divmod(i, SLOTS_G)
                a, b = unit_fields(u)
                if u >= RING:
                    pe.wait_ge(*scaled_before(u - RING, slot))
                elif not (isinstance(slot, int) and slot == 0):
                    pe.wait_ge(*scaled_before(u + UNITS - RING, slot - 1))
                w = slice(a * CROSS, b * CROSS)
                c = slice(j * ROWS, (j + 1) * ROWS)
                dst = ring[u % RING][:, 0:(b - a) * CROSS]
                if j == 0 and u == 0:
                    pe.wait_ge(x1_high, t * GROUPS + g + 1)
                nc.tensor.matmul(dst, x1h[:, g % 2, c], W1h[:, w], start=True, stop=False)
                nc.tensor.matmul(dst, x1h[:, g % 2, c], W1l[:, w], start=False, stop=False)
                if j == 0 and u == 0:
                    pe.wait_ge(x1_low, 2 * (t * GROUPS + g + 1))
                nc.tensor.matmul(dst, x1l[:, g % 2, c], W1h[:, w], start=False, stop=True).then_inc(unit_made, 1)

            def gram_slot(t, i):
                slot = t * SLOTS + i
                pe.wait_ge(x2_summed, 2 * (slot + 1))
                pe.wait_ge(spread_made, slot + 1)
                if not isinstance(slot, int) or slot > 0:
                    pe.wait_ge(gram_copied, slot)
                nc.tensor.matmul(gram_ps[:, 0:(FIELDS + 1) * SLOT_B], x2[:, i % X2_RING, :],
                                 spread[:, i % X2_RING, :, :].rearrange("p f b -> p (f b)"),
                                 start=True, stop=True).then_inc(gram_made, 1)

            def third_layer(t, fields):
                if fields[0] == 0:
                    pe.wait_ge(gram_copied, (t + 1) * SLOTS)
                    pe.wait_ge(w1_in, 32)
                    if isinstance(t, int) and t == TILES - 1:
                        pe.wait_ge(x0r_copied, TILES * GROUPS)
                        pe.wait_ge(s3_copied, 2 * t)
                    else:
                        pe.wait_ge(x0r_copied, (t + 1) * GROUPS + 2)
                for f in fields:
                    mm = nc.tensor.matmul(misc_ps[:, 0:TILE_B], W2[:, f, :], gram[:, f, :],
                                          start=(f == 0), stop=(f == FIELDS - 1))
                if fields[-1] == FIELDS - 1:
                    mm.then_inc(s3_made, 1)

            pe.wait_ge(weights_in, 64)
            turn_emb(0)
            before_x0r(0, 0)
            turn_x0r(0)
            pe.wait_ge(w0_summed, 1)
            first_layer(0, 0)

            def body(t, first, left):
                for i in range(SLOTS):
                    g, j = divmod(i, SLOTS_G)
                    more = g + 1 < GROUPS or left > 0
                    tn, gn = (t, g + 1) if g + 1 < GROUPS else (t + 1, 0)
                    if first and i == 0:
                        pe.wait_ge(w1_low, 1)
                    for u in range(UNITS):
                        if more and j == 1 and u == 2:
                            before_x0r(tn, gn)
                        unit(t, i, u)
                        if more and j == 1 and u == 2:
                            turn_x0r(gn)
                        if more and j == 0 and gn == 0 and u in EMB_TURN_AFTER:
                            turn_emb(tn, [EMB_TURN_AFTER.index(u)])
                        if more and j == SLOTS_G - 1 and u < PAIR_TILES:
                            first_layer(tn, gn, [u])
                        place = (i - LAG) * UNITS + u - 1
                        if not first and 0 <= 4 * place < FIELDS:
                            third_layer(t - 1, range(4 * place, min(4 * place + 4, FIELDS)))
                    if i >= LAG:
                        gram_slot(t, i - LAG)
                    elif not first:
                        gram_slot(t - 1, i - LAG + SLOTS)

            tiles(pe, body)
            for i in range(SLOTS - LAG, SLOTS):
                gram_slot(TILES - 1, i)
            third_layer(TILES - 1, range(FIELDS))

            pe.wait_ge(tower_in, 7 * 16)
            pe.wait_ge(s3_copied, 2 * TILES)
            pe.wait_ge(scalar_scaled, TILES * SLOTS * NS)
            pe.wait_ge(vector_scaled, TILES * SLOTS * NV)
            pe.wait_ge(gram_copied, TILES * SLOTS)
            for h in range(2):
                cols = slice(512 * h, 512 * h + 512)
                for k in range(HID1 // 128):
                    rows = slice(128 * k, 128 * k + 128)
                    if h > 0:
                        pe.wait_ge(hid1_copied, k + 1)
                    for c in range(3):
                        nc.tensor.matmul(ring[k][:], WT1[:, c, rows], S[:, c, cols], start=(c == 0), stop=False)
                    nc.tensor.matmul(ring[k][:], WT1d[:, rows], denseT[:, cols], start=False, stop=True
                                     ).then_inc(hid1_made, 1)
                pe.wait_ge(hid1_copied, 4 * h + 4)
                for k in range(HID2 // 128):
                    if h > 0:
                        pe.wait_ge(hid2_copied, k + 1)
                    for c in range(HID1 // 128):
                        mm = nc.tensor.matmul((x1_ps, gram_ps)[k][:], WT2[:, c, 128 * k:128 * k + 128],
                                              hid1[:, c, cols], start=(c == 0), stop=(c == HID1 // 128 - 1))
                    mm.then_inc(hid2_made, 1)
                pe.wait_ge(hid2_copied, 2 * h + 2)
                if h > 0:
                    pe.wait_ge(y_copied, h)
                for c in range(HID2 // 128):
                    mm = nc.tensor.matmul(misc_ps[0:1, :], WT3[:, c:c + 1], hid2[:, c, cols],
                                          start=(c == 0), stop=(c == HID2 // 128 - 1))
                mm.then_inc(y_made, 1)


def kernel(**inputs):
    import numpy as np
    import concourse.bacc as bacc
    from concourse.bass_utils import run_bass_kernel_spmd

    a = {k: np.asarray(v) for k, v in inputs.items()}
    f0 = a["L0_rec_f0"].reshape(FIELDS, FIELDS, CROSS)
    g = np.arange(FIELDS)
    w0 = np.zeros((2, PER_TILE, FIELDS, PAIR_TILES, CROSS), f0.dtype)
    for i in range(PER_TILE):
        for k in range(PAIR_TILES):
            if k + PAIR_TILES * i < SHIFTS:
                one, other = (g - PAIR_TILES * i) % FIELDS, (g + k) % FIELDS
                w0[0, i, :, k] = f0[one, other]
                if k + i > 0:
                    w0[1, i, :, k] = f0[other, one]
    w0 = w0.reshape(2, PAIR_ROWS, PAIR_TILES, CROSS)

    def by_partition(x, width):
        return x.reshape(-1, 128, width).transpose(1, 0, 2)

    arrays = {
        "ids": a["ids"].reshape(TILES, TILE_B, FIELDS).transpose(1, 0, 2),
        "ident": np.eye(128, dtype=np.float32),
        "block_mask": np.kron(np.eye(SLOT_B, dtype=np.float32), np.ones((DIM, 1), np.float32)),
        "w0a": w0[0], "w0b": w0[1],
        "w1": a["L0_rec_f1"].reshape(FIELDS, CROSS, CROSS).transpose(1, 0, 2),
        "w2": a["L0_rec_f2"].reshape(FIELDS, CROSS, CROSS).transpose(1, 0, 2),
        "dense_t": a["dense_ctx"].T,
        "wt1": by_partition(a["W_top1"][:3 * CROSS], HID1),
        "wt1d": a["W_top1"][3 * CROSS:],
        "bt1": a["b_top1"].reshape(-1, 128).T,
        "wt2": by_partition(a["W_top2"], HID2),
        "bt2": a["b_top2"].reshape(-1, 128).T,
        "wt3": a["W_top3"].reshape(-1, 128).T,
    }
    arrays |= {f"tbl_{f}": a[f"tbl_{f}"] for f in range(FIELDS)}
    arrays = {f"in_{k}": np.ascontiguousarray(v) for k, v in arrays.items()}
    nc = bacc.Bacc("TRN2", target_bir_lowering=False, num_devices=1)
    aps = {k[3:]: nc.dram_tensor(k, v.shape, mybir.dt.from_np(v.dtype), kind="ExternalInput").ap()
           for k, v in arrays.items()}
    tables = [aps.pop(f"tbl_{f}") for f in range(FIELDS)]
    out = nc.dram_tensor("out_y", (1, BATCH), F32, kind="ExternalOutput").ap()
    cin_tower(nc, tables=tables, out=out, **aps)
    r = run_bass_kernel_spmd(nc, [arrays], core_ids=[0])
    return r.results[0]["out_y"].reshape(BATCH, 1)
```

```python
import concourse.bass as bass
from concourse import mybir
from contextlib import ExitStack

F32 = mybir.dt.float32
F32R = mybir.dt.float32r
I32 = mybir.dt.int32
ALU = mybir.AluOpType
ACT = mybir.ActivationFunctionType
AX = mybir.AxisListType

BATCH = 1024
FIELDS = 39
DIM = 16
CROSS = 128
DENSE = 16
HID1 = 512
HID2 = 256
DENSE3 = 64 + DENSE

TILE_B = 128
TILES = BATCH // TILE_B
TILE_COLS = TILE_B * DIM
GROUP_COLS = 512
GROUPS = TILE_COLS // GROUP_COLS
ROWS = 128
SLOTS = TILE_COLS // ROWS
SLOTS_G = SLOTS // GROUPS
SLOT_B = ROWS // DIM

SHIFTS = (FIELDS + 1) // 2
PER_TILE = 3
PAIR_TILES = -(-SHIFTS // PER_TILE)
PAIR_ROWS = PER_TILE * FIELDS
TURNED_ROWS = PAIR_ROWS + PAIR_TILES - 1
SHIFT_DMAS = PER_TILE + PAIR_TILES - 1

UNITS = -(-FIELDS // 4)
RING = 5
VECTOR_UNITS = (2, 5, 8)
SCALAR_UNITS = tuple(u for u in range(UNITS) if u not in VECTOR_UNITS)
ORDER = (*range(1, PAIR_TILES), 0)
DIRECT = 3
SPLIT = PAIR_TILES - DIRECT

PRODUCTS_AT = {
    1: {(0, 0): (0, 1), (0, 2): (2,), (0, 3): (3,), (0, 4): (4, 5), (1, 0): (6,)},
    2: {(4, 2): (0,), (4, 4): (1, 2), (5, 0): (3,), (5, 2): (4,), (5, 4): (5,), (6, 0): (6,)},
    3: {(8, 2): (0,), (8, 4): (1, 2), (9, 0): (3,), (9, 2): (4,), (9, 3): (5,), (10, 0): (6,)},
    0: {(13, 0): (0,), (13, 1): (1,), (13, 2): (2,), (13, 4): (3, 4), (14, 0): (5,), (14, 1): (6,)}}
HIGH_AT = {
    1: {(0, 9): (3,), (1, 1): (4,), (1, 4): (5,), (1, 7): (6,)},
    2: {(5, 6): (3,), (6, 0): (4,), (6, 3): (5,), (6, 6): (6,)},
    3: {(9, 6): (3,), (10, 0): (4,), (10, 3): (5,), (10, 6): (6,)},
    0: {(14, 0): (3,), (14, 1): (4,), (14, 4): (5,), (14, 7): (6,)}}
LOW_AT = {
    1: {(1, 0): (3,), (1, 1): (4,), (1, 2): (5,), (1, 4): (6,)},
    2: {(5, 4): (3,), (6, 1): (4,), (6, 3): (5,), (6, 4): (6,)},
    3: {(9, 4): (3,), (10, 1): (4,), (10, 3): (5,), (10, 4): (6,)},
    0: {(14, 0): (3,), (14, 2): (4,), (14, 3): (5,), (14, 4): (6,)}}
FIRST_LAYER_AT = {
    1: {(0, 5): (0,), (0, 8): (1,), (1, 2): (2,), (1, 5): (3,), (1, 8): (4,), (2, 0): (5,), (2, 3): (6,)},
    2: {(4, 9): (0,), (5, 3): (1,), (5, 7): (2,), (6, 2): (3,), (6, 7): (4,), (7, 0): (5,), (7, 3): (6,)},
    3: {(8, 9): (0,), (9, 3): (1,), (9, 7): (2,), (10, 2): (3,), (10, 7): (4,), (11, 0): (5,), (11, 3): (6,)},
    0: {(13, 6): (0,), (13, 9): (1,), (14, 2): (2,), (14, 4): (3,), (14, 9): (4,), (15, 1): (5,), (15, 3): (6,)}}
HIGH_X1_AT = {1: (2, 6), 2: (7, 4), 3: (11, 4), 0: (15, 4)}
LOW_X1_AT = {1: (2, 3), 2: (7, 2), 3: (11, 2), 0: (15, 2)}
SUM_X1_AT = {1: (2, 4), 2: (7, 4), 3: (11, 4), 0: (15, 4)}
TURN_X0R_AT = {1: (0, 5), 2: (4, 6), 3: (8, 5), 0: (12, 7)}
COPY_X0R_AT = {1: (0, 6), 2: (4, 7), 3: (8, 6), 0: (12, 7)}
TURN_EMB_AT = ((10, 6), (11, 1), (11, 5), (11, 9))
COPY_X0T_AT = ((10, 7), (11, 1), (11, 6), (11, 9))
GRAM_AT = {i: ((i + 2) % SLOTS, 3) for i in range(SLOTS)} | {1: (4, 4), 2: (4, 8)}
COPY_GRAM_AT = {i: ((i + 2) % SLOTS, 6) for i in range(SLOTS)} | {0: (4, 1), 1: (4, 6), 2: (4, 9)}
THIRD_LAYER_FROM = (1, 8)
COPY_S3_AT = (3, 4)
SPLIT_RING = 3
X2_RING = 4

PLACE = {0: 0, 1: 4, 6: 8, 2: 12, 5: 16, 8: 20, 9: 24, 3: 27, 4: 31, 7: 35}
KEPT = 27
HEAD = 12
FOLDS = ((4, 27, 0, 8), (7, 35, 8, 4))


def unit_fields(u):
    return 4 * u, min(4 * u + 4, FIELDS)


def pair_rows(k):
    return len(range(k, SHIFTS, PAIR_TILES)) * FIELDS


def cin_tower(nc, ids, tables, ident, block_mask, w0a, w0b, w1, w2, dense_t, wt1, wt1d, bt1, wt2, bt2, wt3, out):
    with ExitStack() as ctx:
        def sb(name, shape, dt=F32):
            return ctx.enter_context(nc.sbuf_tensor(name, shape, dt))

        def bank(name):
            return ctx.enter_context(nc.psum_tensor(name, [128, 512], F32))

        def sem(name):
            return ctx.enter_context(nc.semaphore(name))

        eye = sb("eye", [128, 128])
        mask = sb("mask", [128, SLOT_B])
        W0h = sb("W0h", [PAIR_ROWS, SPLIT, CROSS], F32R)
        W0l = sb("W0l", [PAIR_ROWS, SPLIT, CROSS], F32R)
        W0 = sb("W0", [PAIR_ROWS, DIRECT, CROSS])
        W1h = sb("W1h", [128, FIELDS * CROSS], F32R)
        W1l = sb("W1l", [128, FIELDS * CROSS], F32R)
        W2 = sb("W2", [128, FIELDS, CROSS])
        BT1 = sb("BT1", [128, HID1 // 128])
        BT2 = sb("BT2", [128, HID2 // 128])
        WT3 = sb("WT3", [128, HID2 // 128])
        idx = sb("idx", [128, FIELDS], I32)
        emb = sb("emb", [128, TURNED_ROWS * DIM])
        x0T = sb("x0T", [128, TILE_COLS])
        pairs_h = sb("pairs_h", [128, SPLIT_RING, GROUP_COLS], F32R)
        pairs_l = sb("pairs_l", [128, SPLIT_RING, GROUP_COLS], F32R)
        x0r = sb("x0r", [128, 2, SLOTS_G, FIELDS + 1])
        x1h = sb("x1h", [128, 2, GROUP_COLS], F32R)
        x1l = sb("x1l", [128, 2, GROUP_COLS], F32R)
        scaled = sb("scaled", [128, 2, FIELDS, CROSS])
        x2 = sb("x2", [128, X2_RING, CROSS])
        spread = sb("spread", [128, X2_RING, FIELDS + 1, SLOT_B])
        gram = sb("gram", [128, FIELDS + 1, TILE_B])
        S = sb("S", [128, 3, BATCH])
        with nc.sbuf_tensor("shifted", [128, 2, PAIR_TILES, GROUP_COLS], F32) as shifted:
            pass

        WT1h = sb("WT1h", [128, 3, HID1], F32R)
        WT1l = sb("WT1l", [128, 3, HID1], F32R)
        WT2h = sb("WT2h", [128, 2, 2 * HID2], F32R)
        WT2l = sb("WT2l", [128, 2, 2 * HID2], F32R)
        dense3 = sb("dense3", [DENSE3, 2, BATCH // 2], F32R)
        WT1d3 = sb("WT1d3", [DENSE3, HID1], F32R)
        dense3_raw = x0T[0:DENSE3, 0:BATCH].rearrange("p (h c) -> p h c", h=2)
        WT1d3_raw = sb("WT1d3_raw", [DENSE3, HID1])
        WT1_raw = emb[:, 0:3 * HID1].rearrange("p (c n) -> p c n", c=3)
        WT2_raw = x0T[:, BATCH:2 * BATCH].rearrange("p (c n) -> p c n", c=2)
        Sh = (pairs_h[:], W1h[:, 0:3 * 512].rearrange("p (c n) -> p c n", c=3))
        Sl = (pairs_l[:], W1l[:, 0:3 * 512].rearrange("p (c n) -> p c n", c=3))
        hid1 = scaled[:, 0, 0:16, :].rearrange("p (k c) m -> p k (c m)", k=HID1 // 128)
        hid2 = scaled[:, 0, 16:24, :].rearrange("p (k c) m -> p k (c m)", k=HID2 // 128)
        hid1h = W1h[:, 3 * 512:3 * 512 + 2048].rearrange("p (k n) -> p k n", k=HID1 // 128)
        hid1l = W1l[:, 3 * 512:3 * 512 + 2048].rearrange("p (k n) -> p k n", k=HID1 // 128)
        y = x2[:, 0, 0:TILES]
        every, low_context, low_weights = slice(0, 128), slice(32, 32 + DENSE), slice(64, 64 + DENSE)
        SPLITS = ([(S[:, c, 0:512], Sh[0][:, c, :], Sl[0][:, c, :], every) for c in range(3)]
                  + [(WT1_raw[:, c, :], WT1h[:, c, :], WT1l[:, c, :], every) for c in range(3)]
                  + [(WT1d3_raw[:], WT1d3[:], WT1d3[low_weights, :], low_weights)]
                  + [(dense3_raw[:, 0, :], dense3[:, 0, :], dense3[low_context, 0, :], low_context)]
                  + [(WT2_raw[:, c, :], WT2h[:, c, :], WT2l[:, c, :], every) for c in range(2)]
                  + [(dense3_raw[:, 1, :], dense3[:, 1, :], dense3[low_context, 1, :], low_context)])
        SPLIT_HIGH_AT = {11: (0, 1), 12: (2, 3), 13: (4, 5, 6), 14: (7, 8), 15: (9, 10)}
        SPLIT_LOW_AT = ((12, 3), (12, 4), (13, 3), (13, 4), (14, 2), (14, 3), (14, 4), (15, 2))

        w0_a = shifted[0:PAIR_ROWS, 0, :, 0:CROSS]
        w0_b = shifted[0:PAIR_ROWS, 1, :, 0:CROSS]

        ring = [bank(f"ring{i}") for i in range(RING)]
        x1_ps = bank("x1_ps")
        misc_ps = bank("misc_ps")
        gram_ps = bank("gram_ps")

        weights_in = sem("weights_in")
        tower_in = sem("tower_in")
        w1_in = sem("w1_in")
        w1_high = sem("w1_high")
        w1_low = sem("w1_low")
        w0_summed = sem("w0_summed")
        w0_high = sem("w0_high")
        w0_low = sem("w0_low")
        ones_set = sem("ones_set")
        idx_in = sem("idx_in")
        gathered = sem("gathered")
        emb_copied = sem("emb_copied")
        emb_turned = sem("emb_turned")
        x0T_copied = sem("x0T_copied")
        shifted_in = [sem("shifted_in0"), sem("shifted_in1")]
        x0r_turned = sem("x0r_turned")
        x0r_copied = sem("x0r_copied")
        products_made = sem("products_made")
        highs_made = sem("highs_made")
        lows_made = sem("lows_made")
        pairs_used = sem("pairs_used")
        x1_high = sem("x1_high")
        x1_low = sem("x1_low")
        unit_made = sem("unit_made")
        scalar_scaled = sem("scalar_scaled")
        vector_scaled = sem("vector_scaled")
        x2_summed = sem("x2_summed")
        folded = sem("folded")
        spread_made = sem("spread_made")
        gram_made = sem("gram_made")
        gram_copied = sem("gram_copied")
        s3_made = sem("s3_made")
        s3_copied = sem("s3_copied")
        hid1_made = sem("hid1_made")
        hid1_copied = sem("hid1_copied")
        hid1_high = sem("hid1_high")
        hid1_low = sem("hid1_low")
        tower_high = sem("tower_high")
        tower_low = sem("tower_low")
        sums_high = sem("sums_high")
        sums_low = sem("sums_low")
        hid2_made = sem("hid2_made")
        hid2_copied = sem("hid2_copied")
        y_made = sem("y_made")
        y_copied = sem("y_copied")
        y_out = sem("y_out")

        NS = len(SCALAR_UNITS)
        NV = len(VECTOR_UNITS)

        def scaled_before(u, slot):
            if u in VECTOR_UNITS:
                return vector_scaled, slot * NV + VECTOR_UNITS.index(u) + 1
            return scalar_scaled, slot * NS + SCALAR_UNITS.index(u) + 1

        E = FIELDS * DIM
        copies = ((emb[:, E:2 * E], emb[:, 0:E]), (emb[:, 2 * E:3 * E], emb[:, 0:E]),
                  (emb[:, 3 * E:TURNED_ROWS * DIM], emb[:, 0:TURNED_ROWS * DIM - 3 * E]))

        def copy_x0T_round(r, bank):
            return (x0T[0:TURNED_ROWS, :].rearrange("f (b d) -> f d b", d=DIM)[:, 4 * r:4 * r + 4, :],
                    bank[0:TURNED_ROWS, :].rearrange("f (d b) -> f d b", d=4))

        def tiles(eng, body):
            body(0, True, 2)
            with eng.Fori(1, TILES - 2) as t:
                body(t, False, 2)
            body(TILES - 2, False, 1)
            body(TILES - 1, False, 0)

        block = ctx.enter_context(nc.Block())

        @block.sync
        def _(sp):
            sp.dma_start(eye[:], ident).then_inc(weights_in, 16)
            sp.dma_start(mask[:], block_mask).then_inc(weights_in, 16)
            sp.dma_start(w0_a, w0a).then_inc(weights_in, 16)
            sp.dma_start(w0_b, w0b).then_inc(weights_in, 16)
            sp.dma_start(W2[:], w1).then_inc(w1_in, 16)

            def shift_group(t, g):
                n = t * GROUPS + g
                p = g % 2
                if g == 0:
                    if isinstance(t, int) and t == 0:
                        sp.wait_ge(w0_low, 2)
                    sp.wait_ge(x0T_copied, (t + 1) * 4)
                elif not (isinstance(n, int) and n < 2):
                    sp.wait_ge(pairs_used, (n - 1) * PAIR_TILES)
                cols = slice(g * GROUP_COLS, (g + 1) * GROUP_COLS)
                for i in range(PER_TILE):
                    start = -PAIR_TILES * i % FIELDS
                    sp.dma_start(shifted[i * FIELDS:(i + 1) * FIELDS, p, 0, :], x0T[start:start + FIELDS, cols]
                                 ).then_inc(shifted_in[p], 16)
                for k in range(1, PAIR_TILES):
                    sp.dma_start(shifted[0:pair_rows(k), p, k, :], x0T[k:k + pair_rows(k), cols]
                                 ).then_inc(shifted_in[p], 16)

            def body(t, first, left):
                for g in range(GROUPS):
                    shift_group(t, g)
                    if first and g == 0:
                        sp.wait_ge(w1_low, 1)
                        sp.dma_start(W2[:], w2).then_inc(w1_in, 16)

            tiles(sp, body)
            sp.wait_ge(pairs_used, TILES * GROUPS * PAIR_TILES)
            for dst, src in ((WT1_raw, wt1), (WT1d3_raw[:], wt1d), (dense3_raw, dense_t), (WT2_raw, wt2),
                             (BT1[:], bt1), (BT2[:], bt2), (WT3[:], wt3)):
                sp.dma_start(dst, src).then_inc(tower_in, 16)
            sp.wait_ge(y_copied, 1)
            sp.dma_start(out, y).then_inc(y_out, 16)
            sp.wait_ge(y_out, 16)

        @block.gpsimd
        def _(pool):
            def load_idx(t):
                if not isinstance(t, int) or t > 0:
                    pool.wait_ge(gathered, t * FIELDS * 16)
                pool.dma_start(idx[:], ids[:, bass.ds(t, 1), :].rearrange("p t f -> p (t f)")
                               if not isinstance(t, int) else ids[:, t, :]).then_inc(idx_in, 16)

            def idx_loaded(t):
                pool.wait_ge(idx_in, (t + 1) * 16)

            def rows_gathered(t):
                pool.wait_ge(gathered, (t + 1) * FIELDS * 16)

            def gather(t, fields):
                for f in fields:
                    pool.indirect_dma_start(
                        emb[:, f * DIM:(f + 1) * DIM], None, tables[f],
                        bass.IndirectOffsetOnAxis(ap=idx[:, f:f + 1], axis=0)).then_inc(gathered, 16)

            def repeat(c):
                pool.tensor_copy(*copies[c]).then_inc(emb_copied, 1)

            def make_spread(t, i):
                slot = t * SLOTS + i
                g, j = divmod(i, SLOTS_G)
                if j == 0:
                    pool.wait_ge(x0r_copied, t * GROUPS + g + 1)
                if not isinstance(slot, int) or slot >= X2_RING:
                    pool.wait_ge(gram_made, slot - X2_RING + 1)
                pool.tensor_tensor(
                    spread[:, i % X2_RING, :, :],
                    x0r[:, g % 2, j, :].unsqueeze(2).to_broadcast([128, FIELDS + 1, SLOT_B]),
                    mask[:].unsqueeze(1).to_broadcast([128, FIELDS + 1, SLOT_B]),
                    ALU.mult).then_inc(spread_made, 1)

            def split_high(numbers):
                for n in numbers:
                    if n == 0:
                        pool.wait_ge(pairs_used, TILES * GROUPS * PAIR_TILES)
                        pool.wait_ge(x1_low, 2 * TILES * GROUPS)
                        pool.wait_ge(s3_copied, TILES)
                    elif n == 3:
                        pool.wait_ge(tower_in, 7 * 16)
                    whole, high = SPLITS[n][0:2]
                    pool.tensor_copy(high, whole).then_inc(tower_high, 1)

            def fold(t, i, n):
                unit, source, onto, k = FOLDS[n]
                slot = t * SLOTS + i
                pool.wait_ge(scalar_scaled, slot * NS + SCALAR_UNITS.index(unit) + 1)
                pool.tensor_tensor(scaled[:, i % 2, onto:onto + k, :], scaled[:, i % 2, onto:onto + k, :],
                                   scaled[:, i % 2, source:source + k, :], ALU.add).then_inc(folded, 1)

            load_idx(0)
            idx_loaded(0)
            gather(0, range(FIELDS - 4))
            pool.memset(x0r[:, :, :, FIELDS:FIELDS + 1], 1.0).then_inc(ones_set, 1)
            gather(0, range(FIELDS - 4, FIELDS))
            pool.wait_ge(emb_turned, 4)
            load_idx(1)
            idx_loaded(1)
            gather(1, range(HEAD))
            pool.wait_ge(weights_in, 64)
            pool.wait_ge(ones_set, 1)

            def body(t, first, left):
                for i in range(SLOTS):
                    if i == 9 and left:
                        rows_gathered(t + 1)
                    if i == 13 and left > 1:
                        idx_loaded(t + 2)
                    make_spread(t, i)
                    if i < 9 and left:
                        gather(t + 1, range(HEAD + 3 * i, HEAD + 3 * i + 3))
                    fold(t, i, 0)
                    if i == 9 and left:
                        repeat(0)
                    fold(t, i, 1)
                    if not left:
                        split_high(SPLIT_HIGH_AT.get(i, ()))
                    if i == 9 and left:
                        repeat(1)
                        repeat(2)
                    if i == 12 and left > 1:
                        pool.wait_ge(emb_turned, (t + 2) * 4)
                        load_idx(t + 2)
                    if i >= 13 and left > 1:
                        gather(t + 2, range(4 * i - 52, 4 * i - 48))

            tiles(pool, body)

        @block.scalar
        def _(act):
            act.wait_ge(w0_summed, 1)
            nc.scalar.activation(W0h[:], w0_a[:, DIRECT:PAIR_TILES, :], ACT.Copy).then_inc(w0_high, 1)
            act.wait_ge(w1_in, 16)
            nc.scalar.activation(W1h[:], W2[:].rearrange("p f m -> p (f m)"), ACT.Copy).then_inc(w1_high, 1)

            def copy_x0T(t, rounds=range(4)):
                for r in rounds:
                    act.wait_ge(emb_turned, t * 4 + r + 1)
                    if r == 0:
                        act.wait_ge(products_made, t * GROUPS * PAIR_TILES)
                        act.wait_ge(shifted_in[1], t * (GROUPS // 2) * SHIFT_DMAS * 16)
                        act.wait_ge(x0r_turned, t * GROUPS)
                    nc.scalar.activation(*copy_x0T_round(r, misc_ps), ACT.Copy).then_inc(x0T_copied, 1)

            def copy_x0r(t, g):
                n = t * GROUPS + g
                act.wait_ge(x0r_turned, n + 1)
                if isinstance(n, int) and n < 2:
                    act.wait_ge(ones_set, 1)
                else:
                    act.wait_ge(vector_scaled, (n - 1) * SLOTS_G * NV)
                    act.wait_ge(spread_made, (n - 1) * SLOTS_G)
                nc.scalar.activation(x0r[:, g % 2, :, 0:FIELDS],
                                     misc_ps[:, 0:SLOTS_G * FIELDS].rearrange("p (j f) -> p j f", f=FIELDS),
                                     ACT.Copy).then_inc(x0r_copied, 1)

            def high_pairs(t, g, numbers):
                n = t * GROUPS + g
                for o in numbers:
                    rows = pair_rows(ORDER[o])
                    act.wait_ge(products_made, n * PAIR_TILES + o + 1)
                    if o == DIRECT and not (isinstance(n, int) and n == 0):
                        act.wait_ge(pairs_used, n * PAIR_TILES)
                    elif o >= DIRECT + SPLIT_RING:
                        act.wait_ge(pairs_used, n * PAIR_TILES + o - SPLIT_RING + 1)
                    nc.scalar.activation(pairs_h[0:rows, (o - DIRECT) % SPLIT_RING, :],
                                         shifted[0:rows, g % 2, ORDER[o], :], ACT.Copy).then_inc(highs_made, 1)

            def high_x1(t, g):
                n = t * GROUPS + g
                act.wait_ge(pairs_used, (n + 1) * PAIR_TILES)
                if not (isinstance(n, int) and n < 2):
                    act.wait_ge(unit_made, (n - 1) * SLOTS_G * UNITS)
                nc.scalar.activation(x1h[:, g % 2, :], x1_ps[:], ACT.Copy).then_inc(x1_high, 1)

            def scale_unit(t, i, u):
                slot = t * SLOTS + i
                g, j = divmod(i, SLOTS_G)
                a, b = unit_fields(u)
                act.wait_ge(unit_made, slot * UNITS + u + 1)
                for f in range(a, b):
                    last = nc.scalar.activation(scaled[:, i % 2, PLACE[u] + f - a, :],
                                                ring[u % RING][:, (f - a) * CROSS:(f - a + 1) * CROSS],
                                                ACT.Copy, scale=x0r[:, g % 2, j, f:f + 1])
                last.then_inc(scalar_scaled, 1)

            def copy_gram(t, i):
                slot = t * SLOTS + i
                act.wait_ge(gram_made, slot + 1)
                if i == 0 and not (isinstance(t, int) and t == 0):
                    act.wait_ge(s3_copied, 2 * t)
                nc.scalar.activation(gram[:, :, i * SLOT_B:(i + 1) * SLOT_B],
                                     gram_ps[:, 0:(FIELDS + 1) * SLOT_B].rearrange("p (f b) -> p f b", b=SLOT_B),
                                     ACT.Copy).then_inc(gram_copied, 1)

            act.wait_ge(gathered, FIELDS * 16)
            for c in (1, 2):
                nc.scalar.activation(*copies[c], ACT.Copy).then_inc(emb_copied, 1)
            for r in (0, 2):
                act.wait_ge(emb_turned, r + 1)
                nc.scalar.activation(*copy_x0T_round(r, ring[r]), ACT.Copy).then_inc(x0T_copied, 1)
            copy_x0r(0, 0)
            high_pairs(0, 0, range(DIRECT, PAIR_TILES))
            high_x1(0, 0)

            def body(t, first, left):
                for i in range(SLOTS):
                    g, j = divmod(i, SLOTS_G)
                    if j == 0:
                        act.wait_ge(x0r_copied, t * GROUPS + g + 1)
                    if not (first and i < 2):
                        act.wait_ge(x2_summed, (t * SLOTS + i - 1) * 2)
                    for u in SCALAR_UNITS:
                        scale_unit(t, i, u)
                        for slot, place in COPY_GRAM_AT.items():
                            if place == (i, u) and slot + 2 < SLOTS:
                                copy_gram(t, slot)
                            elif place == (i, u) and not first:
                                copy_gram(t - 1, slot)
                        for r, place in enumerate(COPY_X0T_AT):
                            if place == (i, u) and left:
                                copy_x0T(t + 1, [r])
                        for gn in range(GROUPS):
                            if gn == 0 and not left:
                                continue
                            tn = t if gn else t + 1
                            if COPY_X0R_AT[gn] == (i, u):
                                copy_x0r(tn, gn)
                            high_pairs(tn, gn, HIGH_AT[gn].get((i, u), ()))
                            if HIGH_X1_AT[gn] == (i, u):
                                high_x1(tn, gn)

            tiles(act, body)
            for i in range(SLOTS - 2, SLOTS):
                copy_gram(TILES - 1, i)

            def hidden1(h):
                for k in range(HID1 // 128):
                    act.wait_ge(hid1_made, 4 * h + k + 1)
                    if h > 0:
                        act.wait_ge(hid1_low, k + 1)
                    nc.scalar.activation(hid1[:, k, :], ring[k][:], ACT.Relu, bias=BT1[:, k:k + 1]
                                         ).then_inc(hid1_copied, 1)

            def hidden2(h):
                for k in range(HID2 // 128):
                    act.wait_ge(hid2_made, 2 * h + k + 1)
                    if h > 0:
                        act.wait_ge(y_made, 1)
                    nc.scalar.activation(hid2[:, k, :], (x1_ps, ring[4])[k][:], ACT.Relu, bias=BT2[:, k:k + 1]
                                         ).then_inc(hid2_copied, 1)

            def high_sums(c, a, b):
                nc.scalar.activation(Sh[1][:, c, a - 512:b - 512], S[:, c, a:b], ACT.Copy).then_inc(sums_high, 1)

            act.wait_ge(x2_summed, 2 * (TILES * SLOTS - 1))
            hidden1(0)
            act.wait_ge(unit_made, TILES * SLOTS * UNITS)
            high_sums(slice(0, 1), 512, BATCH)
            high_sums(slice(1, 3), 512, BATCH - TILE_B)
            hidden2(0)
            act.wait_ge(s3_copied, 2 * TILES)
            high_sums(slice(1, 3), BATCH - TILE_B, BATCH)
            hidden1(1)
            hidden2(1)
            act.wait_ge(y_made, 2)
            nc.scalar.activation(y, gram_ps[:, 0:TILES], ACT.Copy).then_inc(y_copied, 1)

        @block.vector
        def _(dve):
            dve.wait_ge(weights_in, 64)
            whole = slice(0, DIRECT)
            nc.vector.tensor_tensor(W0[:], w0_a[:, whole, :], w0_b[:, whole, :], ALU.add).then_inc(w0_low, 1)
            parts = slice(DIRECT, PAIR_TILES)
            nc.vector.tensor_tensor(w0_a[:, parts, :], w0_a[:, parts, :], w0_b[:, parts, :], ALU.add
                                    ).then_inc(w0_summed, 1)
            dve.wait_ge(w0_high, 1)
            nc.vector.tensor_tensor(W0l[:], w0_a[:, DIRECT:PAIR_TILES, :], W0h[:].bitcast(F32), ALU.subtract
                                    ).then_inc(w0_low, 1)
            dve.wait_ge(w1_high, 1)
            nc.vector.tensor_tensor(W1l[:], W2[:].rearrange("p f m -> p (f m)"), W1h[:].bitcast(F32),
                                    ALU.subtract).then_inc(w1_low, 1)

            def make_products(t, g, numbers):
                n = t * GROUPS + g
                for o in numbers:
                    k = ORDER[o]
                    rows = pair_rows(k)
                    if o == 0:
                        dve.wait_ge(x0T_copied, (t + 1) * 4)
                        dve.wait_ge(shifted_in[g % 2], (t * (GROUPS // 2) + g // 2 + 1) * SHIFT_DMAS * 16)
                    if k == 0:
                        dve.wait_ge(products_made, n * PAIR_TILES + o)
                    second = shifted[0:rows, g % 2, k, :] if k else x0T[0:rows, g * GROUP_COLS:(g + 1) * GROUP_COLS]
                    nc.vector.tensor_tensor(shifted[0:rows, g % 2, k, :], shifted[0:rows, g % 2, 0, :], second,
                                            ALU.mult).then_inc(products_made, 1)

            def low_pairs(t, g, numbers):
                n = t * GROUPS + g
                for o in numbers:
                    rows = pair_rows(ORDER[o])
                    if o == DIRECT and not (isinstance(n, int) and n == 0):
                        dve.wait_ge(pairs_used, n * PAIR_TILES)
                    elif o >= DIRECT + SPLIT_RING:
                        dve.wait_ge(pairs_used, n * PAIR_TILES + o - SPLIT_RING + 1)
                    dve.wait_ge(highs_made, n * SPLIT + o - DIRECT + 1)
                    nc.vector.tensor_tensor(pairs_l[0:rows, (o - DIRECT) % SPLIT_RING, :],
                                            shifted[0:rows, g % 2, ORDER[o], :],
                                            pairs_h[0:rows, (o - DIRECT) % SPLIT_RING, :].bitcast(F32), ALU.subtract
                                            ).then_inc(lows_made, 1)

            def low_x1(t, g):
                n = t * GROUPS + g
                dve.wait_ge(pairs_used, (n + 1) * PAIR_TILES)
                dve.wait_ge(x1_high, n + 1)
                nc.vector.tensor_tensor(x1l[:, g % 2, :], x1_ps[:], x1h[:, g % 2, :].bitcast(F32),
                                        ALU.subtract).then_inc(x1_low, 1)

            def sum_x1(t, g):
                n = t * GROUPS + g
                nb = GROUP_COLS // DIM
                nc.vector.tensor_reduce(S[:, 0, bass.ds(n * nb, nb)],
                                        x1_ps[:].rearrange("p (b d) -> p b d", d=DIM), AX.X, ALU.add
                                        ).then_inc(x1_low, 1)

            def scale_unit(t, i, u):
                slot = t * SLOTS + i
                g, j = divmod(i, SLOTS_G)
                a, b = unit_fields(u)
                if u == VECTOR_UNITS[0] and not (isinstance(slot, int) and slot < 2):
                    dve.wait_ge(x2_summed, 2 * (slot - 1))
                dve.wait_ge(unit_made, slot * UNITS + u + 1)
                nc.vector.tensor_tensor(scaled[:, i % 2, PLACE[u]:PLACE[u] + b - a, :],
                                        ring[u % RING][:, 0:(b - a) * CROSS].rearrange("p (f m) -> p f m", m=CROSS),
                                        x0r[:, g % 2, j, a:b].unsqueeze(2).to_broadcast([128, b - a, CROSS]),
                                        ALU.mult).then_inc(vector_scaled, 1)

            def sum_x2(t, i, half):
                slot = t * SLOTS + i
                if half == 0:
                    dve.wait_ge(scalar_scaled, (slot + 1) * NS)
                    dve.wait_ge(vector_scaled, (slot + 1) * NV)
                    dve.wait_ge(folded, (slot + 1) * len(FOLDS))
                    if not isinstance(slot, int) or slot >= X2_RING:
                        dve.wait_ge(gram_made, slot - X2_RING + 1)
                cols = slice(64 * half, 64 * half + 64)
                nc.vector.tensor_reduce(x2[:, i % X2_RING, cols],
                                        scaled[:, i % 2, 0:KEPT, cols].rearrange("p f m -> p m f"), AX.X, ALU.add
                                        ).then_inc(x2_summed, 1)

            def split_low(n):
                dve.wait_ge(tower_high, n + 1)
                whole, high, low, rows = SPLITS[n]
                nc.vector.tensor_tensor(low, whole[rows, :], high[rows, :].bitcast(F32), ALU.subtract
                                        ).then_inc(tower_low, 1)

            def copy_s3(t):
                dve.wait_ge(s3_made, t + 1)
                cols = bass.ds(t * TILE_B, TILE_B)
                nc.vector.tensor_copy(S[:, 2, cols], misc_ps[:, 0:TILE_B]).then_inc(s3_copied, 1)
                nc.vector.tensor_copy(S[:, 1, cols], gram[:, FIELDS, :]).then_inc(s3_copied, 1)

            dve.wait_ge(gathered, FIELDS * 16)
            nc.vector.tensor_copy(*copies[0]).then_inc(emb_copied, 1)
            for r in (1, 3):
                dve.wait_ge(emb_turned, r + 1)
                nc.vector.tensor_copy(*copy_x0T_round(r, ring[r])).then_inc(x0T_copied, 1)
            make_products(0, 0, range(PAIR_TILES))
            low_pairs(0, 0, range(DIRECT, PAIR_TILES))
            low_x1(0, 0)
            sum_x1(0, 0)

            def body(t, first, left):
                for i in range(SLOTS):
                    g, j = divmod(i, SLOTS_G)
                    if j == 0:
                        dve.wait_ge(x0r_copied, t * GROUPS + g + 1)
                    before = not (first and i == 0)
                    tb, ib = (t, i - 1) if i else (t - 1, SLOTS - 1)
                    for step in range(5):
                        if step in (0, 2, 4):
                            scale_unit(t, i, VECTOR_UNITS[step // 2])
                        elif before:
                            sum_x2(tb, ib, step // 2)
                        if (i, step) == COPY_S3_AT and not first:
                            copy_s3(t - 1)
                        for gn in range(GROUPS):
                            if gn == 0 and not left:
                                continue
                            tn = t if gn else t + 1
                            make_products(tn, gn, PRODUCTS_AT[gn].get((i, step), ()))
                            low_pairs(tn, gn, LOW_AT[gn].get((i, step), ()))
                            if LOW_X1_AT[gn] == (i, step):
                                low_x1(tn, gn)
                            if SUM_X1_AT[gn] == (i, step):
                                sum_x1(tn, gn)
                        if not left and (i, step) in SPLIT_LOW_AT:
                            split_low(SPLIT_LOW_AT.index((i, step)))

            tiles(dve, body)
            sum_x2(TILES - 1, SLOTS - 1, 0)
            sum_x2(TILES - 1, SLOTS - 1, 1)

            for n in range(len(SPLIT_LOW_AT), len(SPLITS)):
                split_low(n)

            def split_hidden1(h):
                for k in range(HID1 // 128):
                    dve.wait_ge(hid1_copied, 4 * h + k + 1)
                    if h > 0:
                        dve.wait_ge(hid2_made, 2)
                    nc.vector.tensor_copy(hid1h[:, k, :], hid1[:, k, :]).then_inc(hid1_high, 1)
                    dve.wait_ge(hid1_high, 4 * h + k + 1)
                    nc.vector.tensor_tensor(hid1l[:, k, :], hid1[:, k, :], hid1h[:, k, :].bitcast(F32),
                                            ALU.subtract).then_inc(hid1_low, 1)

            def low_sums(n, c, a, b):
                dve.wait_ge(sums_high, n)
                nc.vector.tensor_tensor(Sl[1][:, c, a - 512:b - 512], S[:, c, a:b],
                                        Sh[1][:, c, a - 512:b - 512].bitcast(F32), ALU.subtract
                                        ).then_inc(sums_low, 1)

            dve.wait_ge(unit_made, TILES * SLOTS * UNITS)
            split_hidden1(0)
            low_sums(1, slice(0, 1), 512, BATCH)
            low_sums(2, slice(1, 3), 512, BATCH - TILE_B)
            copy_s3(TILES - 1)
            low_sums(3, slice(1, 3), BATCH - TILE_B, BATCH)
            split_hidden1(1)

        @block.tensor
        def _(pe):
            def turn_emb(t, rounds=range(4)):
                by_dim = emb[:].rearrange("p (f d) -> p d f", d=DIM)
                for r in rounds:
                    if r == 0:
                        pe.wait_ge(emb_copied, (t + 1) * len(copies))
                    if isinstance(t, int) and t == 0:
                        bank = ring[r]
                    else:
                        bank = misc_ps
                        if r == 0:
                            pe.wait_ge(x0r_copied, t * GROUPS)
                        else:
                            pe.wait_ge(x0T_copied, t * 4 + r)
                    for q in range(4):
                        mm = nc.tensor.transpose(bank[0:TURNED_ROWS, q * TILE_B:(q + 1) * TILE_B],
                                                 by_dim[:, 4 * r + q, :], eye[:])
                    mm.then_inc(emb_turned, 1)

            def before_x0r(t, g):
                n = t * GROUPS + g
                if g == 0:
                    pe.wait_ge(x0T_copied, (t + 1) * 4)
                else:
                    pe.wait_ge(x0r_copied, n)
                    if g == 2 and not (isinstance(t, int) and t == 0):
                        pe.wait_ge(s3_copied, 2 * t)

            def turn_x0r(g):
                for j in range(SLOTS_G):
                    c = g * GROUP_COLS + j * ROWS
                    mm = nc.tensor.transpose(misc_ps[:, j * FIELDS:(j + 1) * FIELDS],
                                             x0T[0:FIELDS, c:c + ROWS], eye[0:FIELDS, 0:FIELDS])
                mm.then_inc(x0r_turned, 1)

            def first_layer(t, g, o):
                n = t * GROUPS + g
                if o == 0 and not (isinstance(n, int) and n == 0):
                    pe.wait_ge(x1_low, 2 * n)
                k = ORDER[o]
                rows = slice(0, pair_rows(k))
                if o < DIRECT:
                    pe.wait_ge(products_made, n * PAIR_TILES + o + 1)
                    mm = nc.tensor.matmul(x1_ps[:], W0[rows, o, :], shifted[rows, g % 2, k, :],
                                          start=(o == 0), stop=False)
                else:
                    pe.wait_ge(lows_made, n * SPLIT + o - DIRECT + 1)
                    place = (o - DIRECT) % SPLIT_RING
                    high, low = pairs_h[rows, place, :], pairs_l[rows, place, :]
                    nc.tensor.matmul(x1_ps[:], W0h[rows, o - DIRECT, :], high, start=False, stop=False)
                    nc.tensor.matmul(x1_ps[:], W0l[rows, o - DIRECT, :], high, start=False, stop=False)
                    mm = nc.tensor.matmul(x1_ps[:], W0h[rows, o - DIRECT, :], low,
                                          start=False, stop=(o == PAIR_TILES - 1))
                mm.then_inc(pairs_used, 1)

            def unit(t, i, u):
                slot = t * SLOTS + i
                g, j = divmod(i, SLOTS_G)
                a, b = unit_fields(u)
                if u >= RING:
                    pe.wait_ge(*scaled_before(u - RING, slot))
                elif not (isinstance(slot, int) and slot == 0):
                    pe.wait_ge(*scaled_before(u + UNITS - RING, slot - 1))
                w = slice(a * CROSS, b * CROSS)
                c = slice(j * ROWS, (j + 1) * ROWS)
                dst = ring[u % RING][:, 0:(b - a) * CROSS]
                if j == 0 and u == 0:
                    pe.wait_ge(x1_high, t * GROUPS + g + 1)
                nc.tensor.matmul(dst, x1h[:, g % 2, c], W1h[:, w], start=True, stop=False)
                nc.tensor.matmul(dst, x1h[:, g % 2, c], W1l[:, w], start=False, stop=False)
                if j == 0 and u == 0:
                    pe.wait_ge(x1_low, 2 * (t * GROUPS + g) + 1)
                nc.tensor.matmul(dst, x1l[:, g % 2, c], W1h[:, w], start=False, stop=True).then_inc(unit_made, 1)

            def gram_slot(t, i):
                slot = t * SLOTS + i
                pe.wait_ge(x2_summed, 2 * (slot + 1))
                pe.wait_ge(spread_made, slot + 1)
                if not isinstance(slot, int) or slot > 0:
                    pe.wait_ge(gram_copied, slot)
                nc.tensor.matmul(gram_ps[:, 0:(FIELDS + 1) * SLOT_B], x2[:, i % X2_RING, :],
                                 spread[:, i % X2_RING, :, :].rearrange("p f b -> p (f b)"),
                                 start=True, stop=True).then_inc(gram_made, 1)

            def third_layer(t, fields):
                if fields[0] == 0:
                    pe.wait_ge(gram_copied, (t + 1) * SLOTS)
                    pe.wait_ge(w1_in, 32)
                    if isinstance(t, int) and t == TILES - 1:
                        pe.wait_ge(x0r_copied, TILES * GROUPS)
                        pe.wait_ge(s3_copied, 2 * t)
                    else:
                        pe.wait_ge(x0r_copied, (t + 1) * GROUPS + 2)
                for f in fields:
                    mm = nc.tensor.matmul(misc_ps[:, 0:TILE_B], W2[:, f, :], gram[:, f, :],
                                          start=(f == 0), stop=(f == FIELDS - 1))
                if fields[-1] == FIELDS - 1:
                    mm.then_inc(s3_made, 1)

            def keep_warm(n):
                for _ in range(n):
                    nc.tensor.transpose(ring[4][:, 0:128], eye[:], eye[:])

            pe.wait_ge(weights_in, 64)
            pe.wait_ge(ones_set, 1)
            keep_warm(32)
            turn_emb(0)
            before_x0r(0, 0)
            turn_x0r(0)
            keep_warm(64)
            pe.wait_ge(w0_low, 2)
            for o in range(PAIR_TILES):
                first_layer(0, 0, o)

            def body(t, first, left):
                for i in range(SLOTS):
                    if first and i == 0:
                        pe.wait_ge(w1_low, 1)
                    for u in range(UNITS):
                        for gn in range(GROUPS):
                            if TURN_X0R_AT[gn] == (i, u) and (gn or left):
                                before_x0r(t if gn else t + 1, gn)
                        unit(t, i, u)
                        for slot, place in GRAM_AT.items():
                            if place == (i, u) and slot + 2 < SLOTS:
                                gram_slot(t, slot)
                            elif place == (i, u) and not first:
                                gram_slot(t - 1, slot)
                        for r, place in enumerate(TURN_EMB_AT):
                            if place == (i, u) and left:
                                turn_emb(t + 1, [r])
                        for gn in range(GROUPS):
                            if gn == 0 and not left:
                                continue
                            if TURN_X0R_AT[gn] == (i, u):
                                turn_x0r(gn)
                            for o in FIRST_LAYER_AT[gn].get((i, u), ()):
                                first_layer(t if gn else t + 1, gn, o)
                        f = 2 * (i * UNITS + u - THIRD_LAYER_FROM[0] * UNITS - THIRD_LAYER_FROM[1])
                        if not first and 0 <= f < FIELDS:
                            third_layer(t - 1, range(f, min(f + 2, FIELDS)))

            tiles(pe, body)

            def three_passes(dst, wh, wl, xh, xl, start, stop):
                nc.tensor.matmul(dst, wh, xh, start=start, stop=False)
                nc.tensor.matmul(dst, wl, xh, start=False, stop=False)
                return nc.tensor.matmul(dst, wh, xl, start=False, stop=stop)

            def hidden1(h, k):
                rows = slice(128 * k, 128 * k + 128)
                if h == 0:
                    pe.wait_ge(*scaled_before(k + RING, TILES * SLOTS - 1))
                else:
                    pe.wait_ge(hid1_copied, k + 1)
                nc.tensor.matmul(ring[k][:], WT1d3[:, rows], dense3[:, h, :], start=True, stop=False)
                for c in range(3):
                    mm = three_passes(ring[k][:], WT1h[:, c, rows], WT1l[:, c, rows], Sh[h][:, c, :], Sl[h][:, c, :],
                                      False, c == 2)
                mm.then_inc(hid1_made, 1)

            def hidden2(h):
                for k in range(HID2 // 128):
                    if h > 0:
                        pe.wait_ge(hid2_copied, k + 1)
                    for c in range(HID1 // 128):
                        pe.wait_ge(hid1_low, 4 * h + c + 1)
                        cols = slice(256 * (c % 2) + 128 * k, 256 * (c % 2) + 128 * k + 128)
                        mm = three_passes((x1_ps, ring[4])[k][:], WT2h[:, c // 2, cols], WT2l[:, c // 2, cols],
                                          hid1h[:, c, :], hid1l[:, c, :], c == 0, c == HID1 // 128 - 1)
                    mm.then_inc(hid2_made, 1)

            def result(h):
                pe.wait_ge(hid2_copied, 2 * h + 2)
                for b in range(4):
                    for c in range(HID2 // 128):
                        mm = nc.tensor.matmul(gram_ps[:, 4 * h + b:4 * h + b + 1], hid2[:, c, 128 * b:128 * b + 128],
                                              WT3[:, c:c + 1], start=(c == 0), stop=(c == HID2 // 128 - 1))
                mm.then_inc(y_made, 1)

            pe.wait_ge(tower_low, len(SPLIT_LOW_AT))
            hidden1(0, 0)
            gram_slot(TILES - 1, SLOTS - 2)
            hidden1(0, 1)
            hidden1(0, 2)
            gram_slot(TILES - 1, SLOTS - 1)
            hidden1(0, 3)
            third_layer(TILES - 1, range(FIELDS))
            pe.wait_ge(tower_low, len(SPLITS))
            pe.wait_ge(scalar_scaled, TILES * SLOTS * NS)
            hidden2(0)
            result(0)
            pe.wait_ge(sums_low, 3)
            for k in range(4):
                hidden1(1, k)
            hidden2(1)
            result(1)


def kernel(**inputs):
    import numpy as np
    import concourse.bacc as bacc
    from concourse.bass_utils import run_bass_kernel_spmd

    a = {k: np.asarray(v) for k, v in inputs.items()}
    f0 = a["L0_rec_f0"].reshape(FIELDS, FIELDS, CROSS)
    g = np.arange(FIELDS)
    w0 = np.zeros((2, PER_TILE, FIELDS, PAIR_TILES, CROSS), f0.dtype)
    for i in range(PER_TILE):
        for k in range(PAIR_TILES):
            if k + PAIR_TILES * i < SHIFTS:
                one, other = (g - PAIR_TILES * i) % FIELDS, (g + k) % FIELDS
                w0[0, i, :, k] = f0[one, other]
                if k + i > 0:
                    w0[1, i, :, k] = f0[other, one]
    w0 = w0.reshape(2, PAIR_ROWS, PAIR_TILES, CROSS)[:, :, list(ORDER), :]

    def thrice(x):
        t = np.zeros((DENSE3, x.shape[1]), x.dtype)
        t[0:DENSE] = t[32:32 + DENSE] = t[64:64 + DENSE] = x
        return t

    def by_partition(x, width):
        return x.reshape(-1, 128, width).transpose(1, 0, 2)

    arrays = {
        "ids": a["ids"].reshape(TILES, TILE_B, FIELDS).transpose(1, 0, 2),
        "ident": np.eye(128, dtype=np.float32),
        "block_mask": np.kron(np.eye(SLOT_B, dtype=np.float32), np.ones((DIM, 1), np.float32)),
        "w0a": w0[0], "w0b": w0[1],
        "w1": a["L0_rec_f1"].reshape(FIELDS, CROSS, CROSS).transpose(1, 0, 2),
        "w2": a["L0_rec_f2"].reshape(FIELDS, CROSS, CROSS).transpose(1, 0, 2),
        "dense_t": thrice(a["dense_ctx"].T).reshape(DENSE3, 2, BATCH // 2),
        "wt1": by_partition(a["W_top1"][:3 * CROSS], HID1),
        "wt1d": thrice(a["W_top1"][3 * CROSS:]),
        "bt1": a["b_top1"].reshape(-1, 128).T,
        "wt2": by_partition(a["W_top2"], HID2).reshape(128, 2, 2 * HID2),
        "bt2": a["b_top2"].reshape(-1, 128).T,
        "wt3": a["W_top3"].reshape(-1, 128).T,
    }
    arrays |= {f"tbl_{f}": a[f"tbl_{f}"] for f in range(FIELDS)}
    arrays = {f"in_{k}": np.ascontiguousarray(v) for k, v in arrays.items()}
    nc = bacc.Bacc("TRN2", target_bir_lowering=False, num_devices=1)
    aps = {k[3:]: nc.dram_tensor(k, v.shape, mybir.dt.from_np(v.dtype), kind="ExternalInput").ap()
           for k, v in arrays.items()}
    tables = [aps.pop(f"tbl_{f}") for f in range(FIELDS)]
    out = nc.dram_tensor("out_y", (128, TILES), F32, kind="ExternalOutput").ap()
    cin_tower(nc, tables=tables, out=out, **aps)
    r = run_bass_kernel_spmd(nc, [arrays], core_ids=[0])
    return np.ascontiguousarray(r.results[0]["out_y"].T).reshape(BATCH, 1)
```
